# Optimizing a Trainium2 kernel written in Bass

```python
import numpy as np
import jax
import jax.numpy as jnp

def _softmax(x, axis=-1):
    return jax.nn.softmax(x, axis=axis)

def _gelu(x):
    return jax.nn.gelu(x, approximate=True)

def _silu(x):
    return jax.nn.silu(x)

def _sigmoid(x):
    return jax.nn.sigmoid(x)

def _layernorm(x, axis=-1, eps=1e-05):
    m = jnp.mean(x, axis=axis, keepdims=True)
    v = jnp.var(x, axis=axis, keepdims=True)
    return (x - m) / jnp.sqrt(v + eps)

def _scatter_add(tgt, idx, src, axis=0):
    return tgt.at[idx].add(src)

def _segment_sum(src, seg, n):
    return jax.ops.segment_sum(src, seg, n)
kernel_name = 'mk_gnn_preln_d1_gnn_r8_65d0c7'

def setup_inputs(seed: int=0):
    np.random.seed(seed)
    _w = jnp.asarray

    def _rec_inputs():
        import jax
        import jax.numpy as jnp
        _gk = jax.random.key(seed)
        x = -0.0001006 + 1 * jax.random.normal(jax.random.fold_in(_gk, 1), (12500, 96), jnp.float32)
        src = jax.random.randint(jax.random.fold_in(_gk, 2), (200000,), 0, 12500, jnp.int32)
        dst = jnp.minimum((12500 * jax.random.uniform(jax.random.fold_in(_gk, 3), (200000,)) ** 2.0).astype(jnp.int32), 99999)
        _o = jnp.argsort(dst, stable=True)
        src = src[_o]
        dst = dst[_o]
        edge_attr_32 = 0.000196303 + 1.00016 * jax.random.normal(jax.random.fold_in(_gk, 11), (200000, 32), jnp.float32)
        return (x, src, dst, edge_attr_32)
    x, src, dst, edge_attr_32 = _rec_inputs()

    def _L0_gnn_setup():
        import jax, jax.numpy as jnp
        import numpy as np
        N, E = (6250, 100000)
        DIN = DOUT = 96
        DE = 32

        def _egnn_conv(x, src, dst, edge_attr, W_msg, W_edge, W_root, b):
            msg = x[src] @ W_msg + edge_attr @ W_edge
            agg = jax.ops.segment_max(msg, dst, num_segments=x.shape[0])
            agg = jnp.where(jnp.isneginf(agg), 0.0, agg)
            return agg + x @ W_root + b
        key = jax.random.key(seed)
        ks = jax.random.split(key, 10)
        rn = lambda k, sh, sc: jax.random.normal(k, sh, jnp.float32) * sc
        return {'X': rn(ks[0], (N, DIN), 1.0), 'edge_index': jax.random.randint(ks[1], (2, E), 0, N, jnp.int32), 'edge_attr': rn(ks[2], (E, DE), 1.0), 'W1_msg': rn(ks[3], (DIN, DOUT), DIN ** (-0.5)), 'W1_edge': rn(ks[4], (DE, DOUT), DE ** (-0.5)), 'W1_root': rn(ks[5], (DIN, DOUT), DIN ** (-0.5)), 'b1': jnp.zeros((DOUT,), jnp.float32), 'W2_msg': rn(ks[6], (DOUT, DOUT), DOUT ** (-0.5)), 'W2_edge': rn(ks[7], (DE, DOUT), DE ** (-0.5)), 'W2_root': rn(ks[8], (DOUT, DOUT), DOUT ** (-0.5)), 'b2': jnp.zeros((DOUT,), jnp.float32)}
    _L0_gnn_all = _L0_gnn_setup()
    _L0_gnn_in = {k: v for k, v in _L0_gnn_all.items() if k in ('W1_msg', 'W1_edge', 'W1_root', 'b1', 'W2_msg', 'W2_edge', 'W2_root', 'b2')}
    del _L0_gnn_all
    return {'x': x, 'src': src, 'dst': dst, 'edge_attr_32': edge_attr_32, 'L0_gnn_W1_msg': _L0_gnn_in['W1_msg'], 'L0_gnn_W1_edge': _L0_gnn_in['W1_edge'], 'L0_gnn_W1_root': _L0_gnn_in['W1_root'], 'L0_gnn_b1': _L0_gnn_in['b1'], 'L0_gnn_W2_msg': _L0_gnn_in['W2_msg'], 'L0_gnn_W2_edge': _L0_gnn_in['W2_edge'], 'L0_gnn_W2_root': _L0_gnn_in['W2_root'], 'L0_gnn_b2': _L0_gnn_in['b2']}

def reference(x, src, dst, edge_attr_32, L0_gnn_W1_msg, L0_gnn_W1_edge, L0_gnn_W1_root, L0_gnn_b1, L0_gnn_W2_msg, L0_gnn_W2_edge, L0_gnn_W2_root, L0_gnn_b2):
    import jax
    import jax.numpy as jnp

    def _L0_gnn_ref(X, edge_index, edge_attr, W1_msg, W1_edge, W1_root, b1, W2_msg, W2_edge, W2_root, b2):
        import jax, jax.numpy as jnp
        import numpy as np
        N, E = (6250, 100000)
        DIN = DOUT = 96
        DE = 32

        def _egnn_conv(x, src, dst, edge_attr, W_msg, W_edge, W_root, b):
            msg = x[src] @ W_msg + edge_attr @ W_edge
            agg = jax.ops.segment_max(msg, dst, num_segments=x.shape[0])
            agg = jnp.where(jnp.isneginf(agg), 0.0, agg)
            return agg + x @ W_root + b
        src, dst = (edge_index[0], edge_index[1])
        c1 = jax.nn.leaky_relu(_egnn_conv(X, src, dst, edge_attr, W1_msg, W1_edge, W1_root, b1))
        c2 = jax.nn.leaky_relu(_egnn_conv(c1, src, dst, edge_attr, W2_msg, W2_edge, W2_root, b2))
        return c2
    edge_index = jnp.stack([src, dst])
    h = jnp.maximum(_layernorm(x, axis=-1), 0.0)
    x = x + _L0_gnn_ref(h, edge_index, edge_attr_32, L0_gnn_W1_msg, L0_gnn_W1_edge, L0_gnn_W1_root, L0_gnn_b1, L0_gnn_W2_msg, L0_gnn_W2_edge, L0_gnn_W2_root, L0_gnn_b2)
    return x

_drawn_inputs = setup_inputs


def setup_inputs(seed=0):
    import zlib

    import numpy as np

    out = dict(_drawn_inputs(seed))
    spreads = {'L0_gnn_b1': (0.0, 0.267), 'L0_gnn_b2': (0.0, 0.376)}
    factors = {}
    for name, (base, spread) in spreads.items():
        noise = np.random.default_rng([zlib.crc32(name.encode()), seed]).standard_normal(out[name].shape)
        drawn = base * np.exp(spread * noise) if base else spread * noise
        out[name] = jnp.asarray(drawn.astype(out[name].dtype))
    for name, factor in factors.items():
        out[name] = (out[name] * factor).astype(out[name].dtype)
    return out
```

```python
from contextlib import ExitStack

import numpy as np

import concourse.bass as bass
from concourse import mybir

ALU = mybir.AluOpType
ACT = mybir.ActivationFunctionType
AX = mybir.AxisListType
F32 = mybir.dt.float32
BF16 = mybir.dt.bfloat16
I32 = mybir.dt.int32

P = 128
TPB = 4
BLOCK = P * TPB
PAIR = 2 * BLOCK
EPS = 1e-5
SLOPE = 0.01
BIG = 3.3895313892515355e38


def cdiv(a, b):
    return -(-a // b)


def wait(eng, sem, value):
    if isinstance(value, int) and value <= 0:
        return
    eng.wait_ge(sem, value)


def build(nc, x, src_t, dst_t, dst_run, ea_t, weights, out, N, E):
    D = x.shape[1]
    DE = ea_t.shape[1]
    NBLK = x.shape[0] // BLOCK
    NCOL = NBLK * TPB
    EBLK = ea_t.shape[0]
    ECOL = EBLK * TPB
    ITERS = (EBLK - 3) // 4
    LAST_TILES = cdiv(E - (EBLK - 1) * BLOCK, P)
    assert EBLK == 4 * ITERS + 3 and NBLK % 2 == 1 and D == 96 and DE == 32 and NCOL <= P
    NPAIR = cdiv(EBLK, 2)
    GROUP = [(0, 3)] + [(a, min(a + 8, NBLK)) for a in range(3, NBLK, 8)]
    LAST_P = (N - (NBLK - 1) * BLOCK) // TPB
    assert N % TPB == 0

    y_table = nc.dram_tensor("y_table", (NBLK * BLOCK, D), F32, kind="Internal").ap()
    run_table = nc.dram_tensor("run_table", (NPAIR * PAIR, D), F32, kind="Internal").ap()
    mask_table = nc.dram_tensor("mask_table", (EBLK * BLOCK,), BF16, kind="Internal").ap()

    x_v = x.rearrange("(a p t) d -> p a t d", p=P, t=TPB)
    y_v = y_table.rearrange("(a p t) d -> a p (t d)", p=P, t=TPB)
    out_v = out[0:(NBLK - 1) * BLOCK].rearrange("(a p t) d -> a p (t d)", p=P, t=TPB)
    out_last = out[(NBLK - 1) * BLOCK:N].rearrange("(p t) d -> p (t d)", t=TPB)
    run_v = run_table.rearrange("(q p t) d -> q p (t d)", p=P, t=2 * TPB)
    mask_store = mask_table.rearrange("(p c) -> p c", p=P)
    mask_load = mask_table.rearrange("(o e) -> o e", o=1)
    dst_len = EBLK * BLOCK
    dst_prev = dst_run[0:dst_len].rearrange("(p c) -> p c", p=P)
    dst_cur = dst_run[1:dst_len + 1].rearrange("(p c) -> p c", p=P)
    ea_v = ea_t.rearrange("b f e -> (b f) e")

    with ExitStack() as ctx:
        def sb(name, shape, dt):
            return ctx.enter_context(nc.sbuf_tensor(name, shape, dt))

        def banks(name, n):
            return ctx.enter_context(nc.psum_tensor(name, [P, n, BLOCK], F32))

        def sem(name):
            return ctx.enter_context(nc.semaphore(name))

        x_sb = sb("x_sb", [P, NCOL, D], F32)
        root = sb("root", [P, NCOL, D], F32)
        has_edge = sb("has_edge", [P, NCOL], F32)
        end_row = sb("end_row", [P, NCOL], I32)
        ident = sb("ident", [P, P], F32)
        below = sb("below", [P, P], F32)
        ones = sb("ones", [P, P], F32)
        big_row = sb("big_row", [1, D], BF16)
        w_node = [sb(f"w_node{k}", [D + 1, 2 * D], F32) for k in range(2)]
        w_edge = [sb(f"w_edge{k}", [P, D], F32) for k in range(2)]
        dst_p = sb("dst_p", [P, ECOL], BF16)
        dst_c = sb("dst_c", [P, ECOL], BF16)
        dst_a = sb("dst_a", [P, ECOL], I32)
        dst_b = sb("dst_b", [P, ECOL], I32)
        dst_i = sb("dst_i", [P, ECOL], I32)
        mask_sb = sb("mask_sb", [P, ECOL], BF16)
        iota_row = sb("iota_row", [P, P], F32)
        iota_part = sb("iota_part", [P, 1], F32)
        moments = sb("moments", [P, NCOL, 6], F32)
        mean = sb("mean", [P, NCOL], F32)
        diff = sb("diff", [P, NCOL], F32)
        square = sb("square", [P, NCOL], F32)
        std = sb("std", [P, NCOL], F32)
        var = sb("var", [P, NCOL], F32)
        rstd = sb("rstd", [P, NCOL], F32)
        eps = sb("eps", [P, 1], F32)
        feat = [sb(f"feat{s}", [P, TPB, D], F32) for s in range(2)]
        feat_t = [sb(f"feat_t{s}", [D + 1, BLOCK], F32) for s in range(2)]
        y_sb = [sb(f"y_sb{s}", [P, TPB, D], F32) for s in range(2)]
        agg = [sb(f"agg{s}", [P, TPB, D], F32) for s in range(2)]
        work = sb("work", [P, TPB, D], F32)
        idx = [sb(f"idx{p}", [P, 2 * TPB], I32) for p in range(2)]
        ea_sb = sb("ea_sb", [P, BLOCK], F32)
        mask_row = [sb(f"mask_row{p}", [1, PAIR], BF16) for p in range(2)]
        rows = [sb(f"rows{s}", [P, TPB, D], F32) for s in range(4)]
        mask_all = [sb(f"mask_all{b}", [D, BLOCK], BF16) for b in range(2)]
        run = [sb(f"run{b}", [D, BLOCK], F32) for b in range(2)]
        run_rows = [sb(f"run_rows{p}", [P, 2 * TPB, D], F32) for p in range(2)]
        hot_p = [sb(f"hot_p{b}", [P, TPB, P], BF16) for b in range(2)]
        hot_c = [sb(f"hot_c{b}", [P, TPB, NCOL], BF16) for b in range(2)]
        deg = sb("deg", [P, NCOL], F32)
        deg_sum = sb("deg_sum", [P, NBLK], F32)
        through = sb("through", [P, NBLK], F32)
        before = sb("before", [P, NBLK], F32)
        upto = sb("upto", [P, NCOL], F32)
        end_e = sb("end_e", [P, NCOL], I32)
        end_x = sb("end_x", [P, NCOL], I32)
        end_y = sb("end_y", [P, NCOL], I32)

        pair_a, pair_b, pair_c = (banks(n, 2) for n in ("pair_a", "pair_b", "pair_c"))
        ps_count = banks("ps_count", 1)[:, 0, :]
        ps_iota = banks("ps_iota", 1)[:, 0, :]
        ps_msg = ps_turn = [pair_a[:, b, :] for b in range(2)]
        ps_mask = [pair_b[:, b, :] for b in range(2)]
        ps_back = [pair_c[:, b, :] for b in range(2)]
        ps_node = [v[:, :, 0:4 * D].rearrange("p h (t d) -> p h t d", t=2) for v in (pair_b, pair_c)]

        s_x = [sem(f"x_loaded{g}") for g in range(len(GROUP))]
        s_weights = sem("weights_loaded")
        s_dst_runs = sem("dst_runs_loaded")
        s_dst_tiles = sem("dst_tiles_loaded")
        s_iota = sem("iota_made")
        s_const = sem("constants_made")
        s_mask = sem("mask_steps")
        s_mask_stored = sem("mask_stored")
        s_split = sem("dst_split_steps")
        s_moments = sem("moments_made")
        s_stat = sem("statistics_steps")
        s_std = sem("std_made")
        s_rstd = sem("rstd_made")
        s_deg = sem("degree_steps")
        s_deg_sums = sem("degree_sums_made")
        s_fin = sem("output_made")
        s_out = [sem(f"output_stored{s}") for s in range(2)]

        class Nodes:
            def __init__(self, k):
                self.feat_ready = sem(f"feat_ready{k}")
                self.turned = sem(f"turned{k}")
                self.turn_copied = sem(f"turn_copied{k}")
                self.projected = sem(f"projected{k}")
                self.y_copied = sem(f"y_copied{k}")
                self.root_copied = sem(f"root_copied{k}")
                self.y_stored = [sem(f"y_stored{k}_{s}") for s in range(2)]

        class Edges:
            def __init__(self, k):
                self.idx_loaded = [sem(f"idx_loaded{k}_{p}") for p in range(2)]
                self.ea_loaded = [sem(f"ea_loaded{k}_{p}") for p in range(2)]
                self.gathered = [sem(f"gathered{k}_{s}") for s in range(4)]
                self.mask_spread = sem(f"mask_spread{k}")
                self.mask_copied = sem(f"mask_copied{k}")
                self.messages = sem(f"messages{k}")
                self.hot_ready = sem(f"hot_ready{k}")
                self.hot_used = sem(f"hot_used{k}")
                self.scanned = sem(f"scanned{k}")
                self.back = sem(f"back{k}")
                self.back_copied = sem(f"back_copied{k}")
                self.run_stored = [sem(f"run_stored{k}_{p}") for p in range(2)]
                self.end_gathered = [sem(f"end_gathered{k}_{s}") for s in range(2)]
                self.node_steps = sem(f"node_steps{k}")

        POOL_CONSTANTS = 5
        WEIGHT_LOADS = 2 * 7
        STATISTICS_STEPS = 6
        DEGREE_STEPS = 16

        nodes = [Nodes(k) for k in range(2)]
        edges = [Edges(k) for k in range(2)]

        def over_group(eng, step, a0, a1):
            if a0 == 0:
                for a in range(3):
                    step(a, a % 2, a // 2)
                a0 = 3
            if a0 < a1:
                with eng.Fori(a0 // 2, a1 // 2) as i:
                    step(i * 2 + 1, 1, i)
                    step(i * 2 + 2, 0, i + 1)

        def over_nodes(eng, step):
            over_group(eng, step, 0, NBLK)

        def over_edges(eng, step):
            for p in range(2):
                step(0, p, [TPB, TPB])
            with eng.Fori(1, ITERS) as i:
                for p in range(2):
                    step(i, p, [TPB, TPB])
            step(ITERS, 0, [TPB, TPB])
            step(ITERS, 1, [LAST_TILES])

        PAIRS_OF = [cdiv(NPAIR, 2), NPAIR // 2]
        BLOCKS_OF = [cdiv(NBLK, 2), NBLK // 2]

        def columns(v, a):
            return v[:, bass.ds(a * TPB, TPB)]

        block = ctx.enter_context(nc.Block())

        @block.sync
        def _(sp):
            def store_y(k):
                def step(a, s, u):
                    wait(sp, nodes[k].y_copied, a + 1)
                    sp.dma_start(y_v[bass.ds(a, 1)].rearrange("o p f -> (o p) f"),
                                 y_sb[s][:].rearrange("p t d -> p (t d)")).then_inc(nodes[k].y_stored[s], 16)
                return step

            def load_edges(k):
                m = edges[k]

                def step(i, p, tiles):
                    q, n, w = i * 2 + p, i * 4 + 2 * p, len(tiles)
                    for b in range(2):
                        wait(sp, m.gathered[2 * p + b], i * (16 * TPB))
                    sp.dma_start(idx[p][:], src_t[bass.ds(q, 1)].rearrange("o p t -> (o p) t")
                                 ).then_inc(m.idx_loaded[p], 16)
                    wait(sp, m.messages, n - 2)
                    sp.dma_start(ea_sb[2 * p * DE:(2 * p + w) * DE, :],
                                 ea_v[bass.ds(n * DE, w * DE), :]).then_inc(m.ea_loaded[p], 16)
                    sp.dma_start(mask_row[p][:, 0:w * BLOCK],
                                 mask_load[:, bass.ds(n * BLOCK, w * BLOCK)]).then_inc(m.ea_loaded[p], 16)
                return step

            def store_out(a, s, u):
                wait(sp, s_fin, a + 1)
                sp.dma_start(out_v[bass.ds(a, 1)].rearrange("o p f -> (o p) f"),
                             y_sb[s][:].rearrange("p t d -> p (t d)")).then_inc(s_out[s], 16)

            for g, (a0, a1) in enumerate(GROUP):
                sp.dma_start(x_sb[:, TPB * a0:TPB * a1, :].rearrange("p (a t) d -> p a (t d)", t=TPB),
                             x_v[:, a0:a1].rearrange("p a t d -> p a (t d)")).then_inc(s_x[g], 16)
                if g == 1:
                    sp.dma_start(dst_b[:], dst_prev).then_inc(s_dst_runs, 16)
                    sp.dma_start(dst_a[:], dst_cur).then_inc(s_dst_runs, 16)
            sp.dma_start(dst_i[:], dst_t).then_inc(s_dst_tiles, 16)
            over_group(sp, store_y(0), *GROUP[0])
            sp.wait_ge(s_mask, 2)
            sp.dma_start(mask_store, mask_sb[:]).then_inc(s_mask_stored, 16)
            over_group(sp, store_y(0), GROUP[0][1], NBLK)
            sp.wait_ge(s_mask_stored, 16)
            over_edges(sp, load_edges(0))
            over_nodes(sp, store_y(1))
            over_edges(sp, load_edges(1))
            over_group(sp, store_out, 0, NBLK - 2)
            store_out(NBLK - 2, 1, NBLK // 2 - 1)
            sp.wait_ge(s_fin, NBLK)
            sp.dma_start(out_last, y_sb[0][0:LAST_P].rearrange("p t d -> p (t d)")).then_inc(s_out[0], 16)
            for s in range(2):
                sp.wait_ge(s_out[s], 16 * BLOCKS_OF[s])

        @block.gpsimd
        def _(pool):
            def gather(dst, table, index):
                return pool.indirect_dma_start(out=dst, out_offset=None, in_=table,
                                               in_offset=bass.IndirectOffsetOnAxis(ap=index, axis=0))

            def gather_edges(k):
                m = edges[k]

                def step(i, p, tiles):
                    for b, count in enumerate(tiles):
                        s = 2 * p + b
                        if b == 0:
                            wait(pool, m.idx_loaded[p], i * 16 + 16)
                        wait(pool, m.messages, i * 4 + s - 3)
                        pool.nop(nofuse=True)
                        for t in range(count):
                            gather(rows[s][:, t, :], y_table, idx[p][:, t + TPB * b:t + TPB * b + 1]
                                   ).then_inc(m.gathered[s], 16)
                return step

            def gather_ends(k):
                m = edges[k]
                for p in range(2):
                    pool.wait_ge(m.run_stored[p], 16 * PAIRS_OF[p])
                pool.wait_ge(s_deg, DEGREE_STEPS)
                for a in range(NBLK):
                    wait(pool, m.node_steps, (2 + k) * (a - 2) + 1)
                    for t in range(TPB):
                        c = a * TPB + t
                        gather(agg[a % 2][:, t, :], run_table, end_row[:, c:c + 1]).then_inc(m.end_gathered[a % 2], 16)

            pool.iota(iota_row[:], [[1, P]], base=0, channel_multiplier=0,
                      allow_small_or_imprecise_dtypes=True).then_inc(s_iota, 1)
            pool.iota(iota_part[:], [[0, 1]], base=0, channel_multiplier=1,
                      allow_small_or_imprecise_dtypes=True).then_inc(s_iota, 1)
            pool.memset(ones[:], 1.0).then_inc(s_iota, 1)
            pool.memset(big_row[:], BIG).then_inc(s_iota, 1)
            pool.memset(eps[:], EPS).then_inc(s_iota, 1)
            for k in range(2):
                for s in range(2):
                    pool.wait_ge(nodes[k].y_stored[s], 16 * BLOCKS_OF[s])
                over_edges(pool, gather_edges(k))
                gather_ends(k)

        @block.tensor
        def _(pe):
            def project(k):
                m = nodes[k]

                def step(a, s, u):
                    wait(pe, m.feat_ready, a + 1)
                    wait(pe, m.turn_copied, a - 1)
                    for t in range(TPB):
                        mm = pe.transpose(ps_turn[s][0:D, t * P:(t + 1) * P], feat[s][:, t, :], ident[:])
                    mm.then_inc(m.turned, 1)
                    wait(pe, m.turn_copied, a + 1)
                    wait(pe, m.y_copied, a - 1)
                    wait(pe, m.root_copied, a - 1)
                    for t in range(TPB):
                        mm = pe.matmul(ps_node[s][:, t // 2, t % 2, :], feat_t[s][:, t * P:(t + 1) * P],
                                       w_node[k][:], start=True, stop=True)
                    mm.then_inc(m.projected, 1)
                return step

            def form_messages(k):
                m = edges[k]

                def step(i, p, tiles):
                    for b, count in enumerate(tiles):
                        n, w, s = i * 4 + 2 * p + b, count * P, 2 * p + b
                        if b == 0:
                            wait(pe, m.ea_loaded[p], i * 32 + 32)
                        wait(pe, m.mask_copied, n - 1)
                        pe.matmul(ps_mask[b][0:D, 0:w], big_row[:], mask_row[p][:, b * BLOCK:b * BLOCK + w],
                                  start=True, stop=True).then_inc(m.mask_spread, 1)
                        wait(pe, m.scanned, n - 1)
                        wait(pe, m.gathered[s], i * (16 * TPB) + 16 * count)
                        for t in range(count):
                            pe.matmul(ps_msg[b][0:D, t * P:(t + 1) * P], rows[s][:, t, :], ident[:],
                                      is_transpose=True, start=(t == 0), stop=False)
                        pe.matmul(ps_msg[b][0:D, 0:w], w_edge[k][s * DE:(s + 1) * DE, :],
                                  ea_sb[s * DE:(s + 1) * DE, 0:w], start=False, stop=True).then_inc(m.messages, 1)
                    if k == 0:
                        for b, count in enumerate(tiles):
                            n = i * 4 + 2 * p + b
                            wait(pe, m.hot_ready, n + 1)
                            for t in range(count):
                                first = isinstance(n, int) and n == 0 and t == 0
                                last = isinstance(n, int) and n == EBLK - 1 and t == count - 1
                                mm = pe.matmul(ps_count[:, 0:NCOL], hot_p[b][:, t, :], hot_c[b][:, t, :],
                                               start=first, stop=last, skip_group_check=True)
                            mm.then_inc(m.hot_used, 1)
                    for b, count in enumerate(tiles):
                        n = i * 4 + 2 * p + b
                        wait(pe, m.scanned, n + 1)
                        wait(pe, m.back_copied, n - 1)
                        for t in range(count):
                            mm = pe.transpose(ps_back[b][:, t * D:(t + 1) * D], run[b][:, t * P:(t + 1) * P],
                                              ident[0:D, 0:D])
                        mm.then_inc(m.back, 1)
                return step

            pe.wait_ge(s_const, 7)
            pe.wait_ge(s_iota, POOL_CONSTANTS)
            pe.wait_ge(s_weights, 16 * WEIGHT_LOADS)
            for k in range(2):
                over_nodes(pe, project(k))
                pe.wait_ge(nodes[k].y_copied, NBLK)
                pe.wait_ge(nodes[k].root_copied, NBLK)
                over_edges(pe, form_messages(k))
                if k == 0:
                    pe.wait_ge(s_deg, 2)
                    pe.matmul(ps_iota[:, 0:NBLK], below[:], deg_sum[:], start=True, stop=True)
                    pe.matmul(ps_iota[:, P:P + NBLK], ones[:], deg_sum[:], start=True,
                              stop=True).then_inc(s_deg_sums, 1)

        @block.scalar
        def _(act):
            def project(k):
                m = nodes[k]

                def step(a, s, u):
                    wait(act, m.turned, a + 1)
                    wait(act, m.projected, a - 1)
                    act.activation(feat_t[s][0:D, :], ps_turn[s][0:D, :], ACT.Relu if k == 0 else ACT.Copy
                                   ).then_inc(m.turn_copied, 1)
                    wait(act, m.projected, a + 1)
                    wait(act, m.y_stored[s], u * 16)
                    act.activation(y_sb[s][:].rearrange("p (h t) d -> p h t d", h=2), ps_node[s][:, :, :, 0:D],
                                   ACT.Copy).then_inc(m.y_copied, 1)
                    act.activation(columns(root, a).rearrange("p (h t) d -> p h t d", h=2),
                                   ps_node[s][:, :, :, D:2 * D], ACT.Copy).then_inc(m.root_copied, 1)
                return step

            def move_edges(k):
                m = edges[k]

                def step(i, p, tiles):
                    for b, count in enumerate(tiles):
                        n, w = i * 4 + 2 * p + b, count * P
                        wait(act, m.mask_spread, n + 1)
                        wait(act, m.scanned, n - 1)
                        act.activation(mask_all[b][:, 0:w], ps_mask[b][0:D, 0:w], ACT.Copy
                                       ).then_inc(m.mask_copied, 1)
                    wait(act, m.run_stored[p], i * 16)
                    for b, count in enumerate(tiles):
                        n = i * 4 + 2 * p + b
                        wait(act, m.back, n + 1)
                        act.activation(run_rows[p][:, b * TPB:b * TPB + count, :],
                                       ps_back[b][:, 0:count * D].rearrange("p (t d) -> p t d", d=D),
                                       ACT.Copy).then_inc(m.back_copied, 1)
                    wait(act, m.back_copied, i * 4 + 2 * p + len(tiles))
                    act.dma_start(run_v[bass.ds(i * 2 + p, 1)].rearrange("o p f -> (o p) f"),
                                  run_rows[p][:].rearrange("p t d -> p (t d)")).then_inc(m.run_stored[p], 16)
                return step

            for k, (w_msg, w_e, w_root, bias) in enumerate(weights):
                act.dma_start(w_node[k][0:D, 0:D], w_msg).then_inc(s_weights, 16)
                act.dma_start(w_node[k][0:D, D:2 * D], w_root).then_inc(s_weights, 16)
                act.dma_start(w_node[k][D:D + 1, D:2 * D], bias.rearrange("(o d) -> o d", o=1)).then_inc(s_weights, 16)
                for r in range(4):
                    act.dma_start(w_edge[k][r * DE:(r + 1) * DE, :], w_e).then_inc(s_weights, 16)
            def deviation(g):
                a0, a1 = GROUP[g]
                act.wait_ge(s_stat, STATISTICS_STEPS * (g + 1))
                act.activation(std[:, TPB * a0:TPB * a1], var[:, TPB * a0:TPB * a1], ACT.Sqrt,
                               bias=eps[:, 0:1]).then_inc(s_std, 1)

            act.wait_ge(s_iota, POOL_CONSTANTS)
            deviation(0)
            for g, (a0, a1) in enumerate(GROUP):
                if g + 1 < len(GROUP):
                    deviation(g + 1)
                over_group(act, project(0), a0, a1)
            over_edges(act, move_edges(0))
            over_nodes(act, project(1))
            over_edges(act, move_edges(1))

        @block.vector
        def _(dve):
            def chain(sm):
                done = [0]

                def step(ins):
                    done[0] += 1
                    ins.then_inc(sm, 1)
                    dve.wait_ge(sm, done[0])
                return step

            def normalise(a, s, u):
                wait(dve, nodes[0].turned, a - 1)
                for t in range(TPB):
                    c = a * TPB + t
                    ins = dve.tensor_scalar(feat[s][:, t, :], x_sb[:, bass.ds(c, 1), :].rearrange("p o d -> p (o d)"),
                                            mean[:, bass.ds(c, 1)], rstd[:, bass.ds(c, 1)], ALU.subtract, ALU.mult)
                ins.then_inc(nodes[0].feat_ready, 1)

            def scan(k):
                m = edges[k]

                def step(i, p, tiles):
                    for b, count in enumerate(tiles):
                        n, w = i * 4 + 2 * p + b, count * P
                        if k == 0:
                            wait(dve, m.hot_used, n - 1)
                            for hot, of, size in ((hot_p, dst_p, P), (hot_c, dst_c, NCOL)):
                                shape = [P, count, size]
                                ins = dve.tensor_tensor(
                                    hot[b][:, 0:count, :],
                                    ps_iota[:, 0:size].unsqueeze(1).to_broadcast(shape),
                                    of[:, bass.ds(n * TPB, count)].unsqueeze(2).to_broadcast(shape), ALU.is_equal)
                            ins.then_inc(m.hot_ready, 1)
                        wait(dve, m.messages, n + 1)
                        wait(dve, m.mask_copied, n + 1)
                        wait(dve, m.back, n - 1)
                        wait(dve, m.scanned, n)
                        first = isinstance(n, int) and n == 0
                        dve.tensor_tensor_scan(run[b][:, 0:w], mask_all[b][:, 0:w], ps_msg[b][0:D, 0:w],
                                               0.0 if first else run[1 - b][:, BLOCK - 1:BLOCK],
                                               ALU.min, ALU.max).then_inc(m.scanned, 1)
                return step

            def find_ends():
                link = chain(s_deg)
                c_all = ps_count[:, 0:NCOL]
                link(dve.tensor_copy(deg[:], c_all))
                link(dve.tensor_reduce(deg_sum[:], c_all.rearrange("p (a t) -> p a t", t=TPB), AX.X, ALU.add))
                dve.wait_ge(s_deg_sums, 1)
                total = ps_iota[:, P:P + NBLK]
                link(dve.tensor_tensor_scan(through[:], ones[:, 0:NBLK], total, 0.0, ALU.mult, ALU.add))
                link(dve.tensor_tensor(through[:], through[:], total, ALU.subtract))
                link(dve.tensor_tensor(before[:], through[:], ps_iota[:, 0:NBLK], ALU.add))
                deg_v = deg[:].rearrange("p (a t) -> p a t", t=TPB)
                upto_v = upto[:].rearrange("p (a t) -> p a t", t=TPB)
                for t in range(TPB):
                    link(dve.tensor_tensor(upto_v[:, :, t], before[:] if t == 0 else upto_v[:, :, t - 1],
                                           deg_v[:, :, t], ALU.add))
                link(dve.tensor_scalar(end_e[:], upto[:], -1.0, 0.0, ALU.add, ALU.max))
                link(dve.tensor_scalar(has_edge[:], deg[:], 1.0, None, ALU.min))
                link(dve.tensor_scalar(end_x[:], end_e[:], P - 1, 3, ALU.bitwise_and, ALU.logical_shift_left))
                link(dve.tensor_scalar(end_y[:], end_e[:], 7, 7, ALU.logical_shift_right, ALU.bitwise_and))
                link(dve.tensor_scalar(end_e[:], end_e[:], 10, 10, ALU.logical_shift_right, ALU.logical_shift_left))
                link(dve.tensor_tensor(end_x[:], end_x[:], end_y[:], ALU.bitwise_or))
                link(dve.tensor_tensor(end_row[:], end_x[:], end_e[:], ALU.bitwise_or))

            def finish(k):
                m, steps = edges[k], 2 + k

                def step(a, s, u):
                    wait(dve, m.end_gathered[s], u * (16 * TPB) + 16 * TPB)
                    wait(dve, nodes[1].feat_ready if k == 0 else s_fin, a)
                    shape = [P, TPB, D]
                    dve.tensor_tensor(work[:], agg[s][:], columns(has_edge, a).unsqueeze(2).to_broadcast(shape),
                                      ALU.mult).then_inc(m.node_steps, 1)
                    wait(dve, m.node_steps, a * steps + 1)
                    dve.tensor_tensor(work[:], work[:], columns(root, a), ALU.add).then_inc(m.node_steps, 1)
                    wait(dve, m.node_steps, a * steps + 2)
                    if k == 0:
                        wait(dve, nodes[1].turned, a - 1)
                    ins = dve.scalar_tensor_tensor(out=feat[s][:], in0=work[:], scalar=SLOPE, in1=work[:],
                                                   op0=ALU.mult, op1=ALU.max)
                    if k == 0:
                        ins.then_inc(nodes[1].feat_ready, 1)
                    else:
                        ins.then_inc(m.node_steps, 1)
                        wait(dve, m.node_steps, a * steps + 3)
                        wait(dve, s_out[s], u * 16)
                        dve.tensor_tensor(y_sb[s][:], feat[s][:], columns(x_sb, a), ALU.add).then_inc(s_fin, 1)
                return step

            for s in range(2):
                dve.memset(feat_t[s][D:D + 1, :], 1.0).then_inc(s_const, 1)
                dve.memset(w_node[s][D:D + 1, 0:D], 0.0).then_inc(s_const, 1)
            dve.wait_ge(s_iota, POOL_CONSTANTS)
            dve.tensor_scalar(ident[:], iota_row[:], iota_part[:, 0:1], None, ALU.is_equal).then_inc(s_const, 1)
            dve.tensor_scalar(below[:], iota_row[:], iota_part[:, 0:1], None, ALU.is_gt).then_inc(s_const, 1)
            dve.tensor_copy(ps_iota[:, 0:P], iota_row[:]).then_inc(s_const, 1)

            stat_link = chain(s_stat)

            def statistics(g):
                a0, a1 = GROUP[g]
                dve.wait_ge(s_x[g], 16)
                with dve.Fori(a0, a1) as a:
                    for t in range(TPB):
                        ins = dve.bn_stats(moments[:, bass.ds(a * TPB + t, 1), :].rearrange("p o f -> p (o f)"),
                                           x_sb[:, bass.ds(a * TPB + t, 1), :].rearrange("p o d -> p (o d)"))
                    ins.then_inc(s_moments, 1)
                dve.wait_ge(s_moments, a1)
                cols = slice(TPB * a0, TPB * a1)
                mom = moments[:, cols, :]
                mean_e, m2_e, mean_o, m2_o = (mom[:, :, f] for f in (1, 2, 4, 5))
                mn, df, sq, vr = (v[:, cols] for v in (mean, diff, square, var))
                stat_link(dve.tensor_tensor(mn, mean_e, mean_o, ALU.add))
                stat_link(dve.tensor_scalar(mn, mn, 0.5, None, ALU.mult))
                stat_link(dve.tensor_tensor(df, mean_e, mean_o, ALU.subtract))
                stat_link(dve.scalar_tensor_tensor(out=sq, in0=df, scalar=0.25, in1=df, op0=ALU.mult, op1=ALU.mult))
                stat_link(dve.tensor_tensor(vr, m2_e, m2_o, ALU.add))
                stat_link(dve.scalar_tensor_tensor(out=vr, in0=vr, scalar=1.0 / D, in1=sq, op0=ALU.mult, op1=ALU.add))

            statistics(0)
            for g, (a0, a1) in enumerate(GROUP):
                if g + 1 < len(GROUP):
                    statistics(g + 1)
                cols = slice(TPB * a0, TPB * a1)
                dve.wait_ge(s_std, g + 1)
                dve.reciprocal(rstd[:, cols], std[:, cols]).then_inc(s_rstd, 1)
                dve.wait_ge(s_rstd, g + 1)
                over_group(dve, normalise, a0, a1)
                if g == 0:
                    dve.wait_ge(s_dst_runs, 32)
                    dve.tensor_tensor(mask_sb[:], dst_b[:], dst_a[:], ALU.is_equal).then_inc(s_mask, 1)
                    dve.wait_ge(s_mask, 1)
                    dve.tensor_scalar(mask_sb[:], mask_sb[:], 2.0, -1.0, ALU.mult, ALU.add).then_inc(s_mask, 1)

            dve.wait_ge(s_dst_tiles, 16)
            dve.wait_ge(s_mask_stored, 16)
            link = chain(s_split)
            link(dve.tensor_scalar(dst_a[:], dst_i[:], 2, P - 1, ALU.logical_shift_right, ALU.bitwise_and))
            link(dve.tensor_copy(dst_p[:], dst_a[:]))
            link(dve.tensor_scalar(dst_b[:], dst_i[:], 9, 2, ALU.logical_shift_right, ALU.logical_shift_left))
            link(dve.tensor_scalar(dst_a[:], dst_i[:], TPB - 1, None, ALU.bitwise_and))
            link(dve.tensor_tensor(dst_c[:], dst_a[:], dst_b[:], ALU.add))

            over_edges(dve, scan(0))
            dve.wait_ge(edges[0].hot_used, EBLK)
            find_ends()
            over_nodes(dve, finish(0))
            over_edges(dve, scan(1))
            over_nodes(dve, finish(1))


def kernel(**inputs):
    import concourse.bacc as bacc
    from concourse.bass_utils import run_bass_kernel_spmd

    a = {n: np.ascontiguousarray(v) for n, v in inputs.items()}
    x, src, dst, ea = a["x"], a["src"], a["dst"], a["edge_attr_32"]
    N, D = x.shape
    E, DE = ea.shape
    nblk, eblk = cdiv(N, BLOCK), cdiv(E, BLOCK)
    npair = cdiv(eblk, 2)

    x_pad = np.zeros((nblk * BLOCK, D), x.dtype)
    x_pad[:N] = x
    src_pad = np.zeros(npair * PAIR, src.dtype)
    src_pad[:E] = src
    dst_run = np.full(1 + eblk * BLOCK, N, dst.dtype)
    dst_run[0] = -1
    dst_run[1:E + 1] = dst
    ea_pad = np.zeros((eblk * BLOCK, DE), ea.dtype)
    ea_pad[:E] = ea
    arrays = {
        "x_pad": x_pad,
        "src_tiles": np.ascontiguousarray(src_pad.reshape(npair, 2 * TPB, P).transpose(0, 2, 1)),
        "dst_tiles": np.ascontiguousarray(dst_run[1:].reshape(eblk * TPB, P).T),
        "dst_run": dst_run,
        "edge_attr_t": np.ascontiguousarray(ea_pad.reshape(eblk, BLOCK, DE).transpose(0, 2, 1)),
    }
    names = [[f"L0_gnn_{w}" for w in (f"W{k}_msg", f"W{k}_edge", f"W{k}_root", f"b{k}")] for k in (1, 2)]
    arrays |= {n: a[n] for layer in names for n in layer}

    nc = bacc.Bacc("TRN2", target_bir_lowering=False, num_devices=1)
    aps = {n: nc.dram_tensor(n, v.shape, mybir.dt.from_np(v.dtype), kind="ExternalInput").ap()
           for n, v in arrays.items()}
    out = nc.dram_tensor("out", (N, D), F32, kind="ExternalOutput").ap()
    build(nc, aps["x_pad"], aps["src_tiles"], aps["dst_tiles"], aps["dst_run"], aps["edge_attr_t"],
          [[aps[n] for n in layer] for layer in names], out, N, E)
    r = run_bass_kernel_spmd(nc, [{n: v for n, v in arrays.items()}], core_ids=[0])
    return r.results[0]["out"]
```

```python
from contextlib import ExitStack

import numpy as np

import concourse.bass as bass
from concourse import mybir

ALU = mybir.AluOpType
ACT = mybir.ActivationFunctionType
AX = mybir.AxisListType
F32 = mybir.dt.float32
BF16 = mybir.dt.bfloat16
I32 = mybir.dt.int32

P = 128
TPB = 4
BLOCK = P * TPB
PAIR = 2 * BLOCK
EPS = 1e-5
SLOPE = 0.01
BIG = 3.3895313892515355e38


def cdiv(a, b):
    return -(-a // b)


def wait(eng, sem, value):
    if isinstance(value, int) and value <= 0:
        return
    eng.wait_ge(sem, value)


def build(nc, x, src_t, dst_t, dst_run, ea_t, weights, out, N, E):
    D = x.shape[1]
    DE = ea_t.shape[1]
    NBLK = x.shape[0] // BLOCK
    NCOL = NBLK * TPB
    EBLK = ea_t.shape[0]
    ECOL = EBLK * TPB
    ITERS = (EBLK - 3) // 4
    LAST_TILES = cdiv(E - (EBLK - 1) * BLOCK, P)
    assert EBLK == 4 * ITERS + 3 and NBLK % 2 == 1 and D == 96 and DE == 32 and NCOL <= P
    NPAIR = cdiv(EBLK, 2)
    GROUP_MAX = 3
    GROUP = [(a, min(a + GROUP_MAX, NBLK)) for a in range(0, NBLK, GROUP_MAX)]
    LAST_P = (N - (NBLK - 1) * BLOCK) // TPB
    assert N % TPB == 0

    y_table = nc.dram_tensor("y_table", (NBLK * BLOCK, D), F32, kind="Internal").ap()
    run_table = nc.dram_tensor("run_table", (NPAIR * PAIR, D), F32, kind="Internal").ap()
    mask_table = nc.dram_tensor("mask_table", (EBLK * BLOCK,), BF16, kind="Internal").ap()

    x_v = x.rearrange("(a p t) d -> p a t d", p=P, t=TPB)
    y_v = y_table.rearrange("(a p t) d -> a p (t d)", p=P, t=TPB)
    out_v = out[0:(NBLK - 1) * BLOCK].rearrange("(a p t) d -> a p (t d)", p=P, t=TPB)
    out_last = out[(NBLK - 1) * BLOCK:N].rearrange("(p t) d -> p (t d)", t=TPB)
    run_v = run_table.rearrange("(q p t) d -> q p (t d)", p=P, t=2 * TPB)
    mask_store = mask_table.rearrange("(p c) -> p c", p=P)
    mask_load = mask_table.rearrange("(o e) -> o e", o=1)
    dst_len = EBLK * BLOCK
    dst_prev = dst_run[0:dst_len].rearrange("(p c) -> p c", p=P)
    dst_cur = dst_run[1:dst_len + 1].rearrange("(p c) -> p c", p=P)
    ea_v = ea_t.rearrange("b f e -> (b f) e")

    with ExitStack() as ctx:
        def sb(name, shape, dt):
            return ctx.enter_context(nc.sbuf_tensor(name, shape, dt))

        def banks(name, n):
            return ctx.enter_context(nc.psum_tensor(name, [P, n, BLOCK], F32))

        def sem(name):
            return ctx.enter_context(nc.semaphore(name))

        x_sb = sb("x_sb", [P, NCOL, D], F32)
        root = sb("root", [P, NCOL, D], F32)
        has_edge = sb("has_edge", [P, NCOL], F32)
        end_row = sb("end_row", [P, NCOL], I32)
        ident = sb("ident", [P, P], F32)
        below = sb("below", [P, P], F32)
        ones = sb("ones", [P, P], F32)
        big_row = sb("big_row", [1, D], BF16)
        w_node = [sb(f"w_node{k}", [D + 1, 2 * D], F32) for k in range(2)]
        w_edge = [sb(f"w_edge{k}", [P, D], F32) for k in range(2)]
        dst_p = sb("dst_p", [P, ECOL], BF16)
        dst_c = sb("dst_c", [P, ECOL], BF16)
        dst_a = sb("dst_a", [P, ECOL], I32)
        dst_b = sb("dst_b", [P, ECOL], I32)
        dst_i = sb("dst_i", [P, ECOL], I32)
        mask_sb = sb("mask_sb", [P, ECOL], BF16)
        iota_row = sb("iota_row", [P, P], F32)
        iota_part = sb("iota_part", [P, 1], F32)
        mean = sb("mean", [P, NCOL], F32)
        square = [sb(f"square{j}", [P, TPB * GROUP_MAX, D], F32) for j in range(2)]
        square_sum = sb("square_sum", [P, NCOL], F32)
        std = sb("std", [P, NCOL], F32)
        rstd = sb("rstd", [P, NCOL], F32)
        eps = sb("eps", [P, 1], F32)
        feat = [sb(f"feat{s}", [P, TPB, D], F32) for s in range(2)]
        feat_t = [sb(f"feat_t{s}", [D + 1, BLOCK], F32) for s in range(2)]
        y_sb = [sb(f"y_sb{s}", [P, TPB, D], F32) for s in range(2)]
        agg = [sb(f"agg{s}", [P, TPB, D], F32) for s in range(2)]
        work = sb("work", [P, TPB, D], F32)
        idx = [sb(f"idx{p}", [P, 2 * TPB], I32) for p in range(2)]
        ea_sb = sb("ea_sb", [P, BLOCK], F32)
        mask_row = [sb(f"mask_row{p}", [1, PAIR], BF16) for p in range(2)]
        rows = [sb(f"rows{s}", [P, TPB, D], F32) for s in range(4)]
        mask_all = [sb(f"mask_all{b}", [D, BLOCK], BF16) for b in range(2)]
        run = [sb(f"run{b}", [D, BLOCK], F32) for b in range(2)]
        run_rows = [sb(f"run_rows{p}", [P, 2 * TPB, D], F32) for p in range(2)]
        hot_p = [sb(f"hot_p{b}", [P, TPB, P], BF16) for b in range(2)]
        hot_c = [sb(f"hot_c{b}", [P, TPB, NCOL], BF16) for b in range(2)]
        deg = sb("deg", [P, NCOL], F32)
        deg_sum = sb("deg_sum", [P, NBLK], F32)
        through = sb("through", [P, NBLK], F32)
        before = sb("before", [P, NBLK], F32)
        upto = sb("upto", [P, NCOL], F32)
        end_e = sb("end_e", [P, NCOL], I32)
        end_x = sb("end_x", [P, NCOL], I32)
        end_y = sb("end_y", [P, NCOL], I32)

        pair_a, pair_b, pair_c = (banks(n, 2) for n in ("pair_a", "pair_b", "pair_c"))
        ps_count = banks("ps_count", 1)[:, 0, :]
        ps_iota = banks("ps_iota", 1)[:, 0, :]
        ps_msg = ps_turn = [pair_a[:, b, :] for b in range(2)]
        ps_mask = [pair_b[:, b, :] for b in range(2)]
        ps_back = [pair_c[:, b, :] for b in range(2)]
        ps_node = [v[:, :, 0:4 * D].rearrange("p h (t d) -> p h t d", t=2) for v in (pair_b, pair_c)]

        s_x = [sem(f"x_loaded{g}") for g in range(len(GROUP))]
        s_weights = [sem(f"node_weights_loaded{k}") for k in range(2)]
        s_w_edge = [sem(f"edge_weights_loaded{k}") for k in range(2)]
        s_dst_runs = sem("dst_runs_loaded")
        s_dst_tiles = sem("dst_tiles_loaded")
        s_iota = sem("iota_made")
        s_const = sem("constants_made")
        s_mask = sem("mask_steps")
        s_mask_stored = sem("mask_stored")
        s_split = sem("dst_split_steps")
        s_sum = sem("sums_made")
        s_mean = sem("means_made")
        s_centered = sem("centered")
        s_squared = sem("squared")
        s_square_sum = sem("square_sums_made")
        s_std = sem("std_made")
        s_rstd = sem("rstd_made")
        s_deg = sem("degree_steps")
        s_deg_sums = sem("degree_sums_made")
        s_fin = sem("output_made")
        s_out = [sem(f"output_stored{s}") for s in range(2)]

        class Nodes:
            def __init__(self, k):
                self.feat_ready = sem(f"feat_ready{k}")
                self.turned = sem(f"turned{k}")
                self.turn_copied = sem(f"turn_copied{k}")
                self.projected = sem(f"projected{k}")
                self.y_copied = sem(f"y_copied{k}")
                self.root_copied = sem(f"root_copied{k}")
                self.y_stored = [sem(f"y_stored{k}_{s}") for s in range(2)]

        class Edges:
            def __init__(self, k):
                self.idx_loaded = [sem(f"idx_loaded{k}_{p}") for p in range(2)]
                self.ea_loaded = [sem(f"ea_loaded{k}_{p}") for p in range(2)]
                self.gathered = [sem(f"gathered{k}_{s}") for s in range(4)]
                self.mask_spread = sem(f"mask_spread{k}")
                self.mask_copied = sem(f"mask_copied{k}")
                self.messages = sem(f"messages{k}")
                self.hot_ready = sem(f"hot_ready{k}")
                self.hot_used = sem(f"hot_used{k}")
                self.scanned = sem(f"scanned{k}")
                self.back = sem(f"back{k}")
                self.back_copied = sem(f"back_copied{k}")
                self.run_stored = [sem(f"run_stored{k}_{p}") for p in range(2)]
                self.end_gathered = [sem(f"end_gathered{k}_{s}") for s in range(2)]
                self.node_steps = sem(f"node_steps{k}")

        LAG = 2
        POOL_CONSTANTS = 5
        DEGREE_STEPS = 16

        nodes = [Nodes(k) for k in range(2)]
        edges = [Edges(k) for k in range(2)]

        def over_group(eng, step, a0, a1):
            for a in range(a0, min(a1, 3)):
                step(a, a % 2, a // 2)
            a0 = max(a0, 3)
            if a0 < a1:
                with eng.Fori(a0 // 2, a1 // 2) as i:
                    step(i * 2 + 1, 1, i)
                    step(i * 2 + 2, 0, i + 1)

        def over_nodes(eng, step):
            over_group(eng, step, 0, NBLK)

        def over_edges(eng, step):
            for p in range(2):
                step(0, p, [TPB, TPB])
            with eng.Fori(1, ITERS) as i:
                for p in range(2):
                    step(i, p, [TPB, TPB])
            step(ITERS, 0, [TPB, TPB])
            step(ITERS, 1, [LAST_TILES])

        PAIRS_OF = [cdiv(NPAIR, 2), NPAIR // 2]
        BLOCKS_OF = [cdiv(NBLK, 2), NBLK // 2]

        def columns(v, a):
            return v[:, bass.ds(a * TPB, TPB)]

        def columns_of(g):
            return slice(TPB * GROUP[g][0], TPB * GROUP[g][1])

        block = ctx.enter_context(nc.Block())

        @block.sync
        def _(sp):
            def load_weights(k):
                w_msg, w_e, w_root, bias = weights[k]
                sp.dma_start(w_node[k][0:D, 0:D], w_msg).then_inc(s_weights[k], 16)
                sp.dma_start(w_node[k][0:D, D:2 * D], w_root).then_inc(s_weights[k], 16)
                sp.dma_start(w_node[k][D:D + 1, D:2 * D], bias.rearrange("(o d) -> o d", o=1)).then_inc(s_weights[k], 16)
                for r in range(4):
                    sp.dma_start(w_edge[k][r * DE:(r + 1) * DE, :], w_e).then_inc(s_w_edge[k], 16)

            def store_y(k):
                def step(a, s, u):
                    wait(sp, nodes[k].y_copied, a + 1)
                    sp.dma_start(y_v[bass.ds(a, 1)].rearrange("o p f -> (o p) f"),
                                 y_sb[s][:].rearrange("p t d -> p (t d)")).then_inc(nodes[k].y_stored[s], 16)
                return step

            def load_edges(k):
                m = edges[k]

                def step(i, p, tiles):
                    q, n, w = i * 2 + p, i * 4 + 2 * p, len(tiles)
                    for b in range(2):
                        wait(sp, m.gathered[2 * p + b], i * (16 * TPB))
                    sp.dma_start(idx[p][:], src_t[bass.ds(q, 1)].rearrange("o p t -> (o p) t")
                                 ).then_inc(m.idx_loaded[p], 16)
                    wait(sp, m.messages, n - 2)
                    sp.dma_start(ea_sb[2 * p * DE:(2 * p + w) * DE, :],
                                 ea_v[bass.ds(n * DE, w * DE), :]).then_inc(m.ea_loaded[p], 16)
                    sp.dma_start(mask_row[p][:, 0:w * BLOCK],
                                 mask_load[:, bass.ds(n * BLOCK, w * BLOCK)]).then_inc(m.ea_loaded[p], 16)
                return step

            def store_out(a, s, u):
                wait(sp, s_fin, a + 1)
                sp.dma_start(out_v[bass.ds(a, 1)].rearrange("o p f -> (o p) f"),
                             y_sb[s][:].rearrange("p t d -> p (t d)")).then_inc(s_out[s], 16)

            for g, (a0, a1) in enumerate(GROUP):
                sp.dma_start(x_sb[:, TPB * a0:TPB * a1, :].rearrange("p (a t) d -> p a (t d)", t=TPB),
                             x_v[:, a0:a1].rearrange("p a t d -> p a (t d)")).then_inc(s_x[g], 16)
            load_weights(0)
            sp.dma_start(dst_b[:], dst_prev).then_inc(s_dst_runs, 16)
            sp.dma_start(dst_a[:], dst_cur).then_inc(s_dst_runs, 16)
            sp.dma_start(dst_i[:], dst_t).then_inc(s_dst_tiles, 16)
            load_weights(1)
            over_group(sp, store_y(0), 0, 7)
            sp.wait_ge(s_mask, 2)
            sp.dma_start(mask_store, mask_sb[:]).then_inc(s_mask_stored, 16)
            over_group(sp, store_y(0), 7, NBLK)
            sp.wait_ge(s_mask_stored, 16)
            over_edges(sp, load_edges(0))
            over_nodes(sp, store_y(1))
            over_edges(sp, load_edges(1))
            over_group(sp, store_out, 0, NBLK - 2)
            store_out(NBLK - 2, 1, NBLK // 2 - 1)
            sp.wait_ge(s_fin, NBLK)
            sp.dma_start(out_last, y_sb[0][0:LAST_P].rearrange("p t d -> p (t d)")).then_inc(s_out[0], 16)
            for s in range(2):
                sp.wait_ge(s_out[s], 16 * BLOCKS_OF[s])

        @block.gpsimd
        def _(pool):
            def gather(dst, table, index):
                return pool.indirect_dma_start(out=dst, out_offset=None, in_=table,
                                               in_offset=bass.IndirectOffsetOnAxis(ap=index, axis=0))

            def gather_edges(k):
                m = edges[k]

                def step(i, p, tiles):
                    for b, count in enumerate(tiles):
                        s = 2 * p + b
                        if b == 0:
                            wait(pool, m.idx_loaded[p], i * 16 + 16)
                        wait(pool, m.messages, i * 4 + s - 3)
                        pool.nop(nofuse=True)
                        for t in range(count):
                            gather(rows[s][:, t, :], y_table, idx[p][:, t + TPB * b:t + TPB * b + 1]
                                   ).then_inc(m.gathered[s], 16)
                return step

            def gather_ends(k):
                m = edges[k]
                for p in range(2):
                    pool.wait_ge(m.run_stored[p], 16 * PAIRS_OF[p])
                pool.wait_ge(s_deg, DEGREE_STEPS)
                for a in range(NBLK):
                    wait(pool, m.node_steps, (2 + k) * (a - 2) + 1)
                    for t in range(TPB):
                        c = a * TPB + t
                        gather(agg[a % 2][:, t, :], run_table, end_row[:, c:c + 1]).then_inc(m.end_gathered[a % 2], 16)

            pool.iota(iota_row[:], [[1, P]], base=0, channel_multiplier=0,
                      allow_small_or_imprecise_dtypes=True).then_inc(s_iota, 1)
            pool.iota(iota_part[:], [[0, 1]], base=0, channel_multiplier=1,
                      allow_small_or_imprecise_dtypes=True).then_inc(s_iota, 1)
            pool.memset(ones[:], 1.0).then_inc(s_iota, 1)
            pool.memset(big_row[:], BIG).then_inc(s_iota, 1)
            pool.memset(eps[:], EPS).then_inc(s_iota, 1)
            for g in range(len(GROUP)):
                cols = columns_of(g)
                pool.wait_ge(s_mean, g + 1)
                shape = [P, cols.stop - cols.start, D]
                pool.tensor_tensor(root[:, cols, :], x_sb[:, cols, :], mean[:, cols].unsqueeze(2).to_broadcast(shape),
                                   ALU.subtract).then_inc(s_centered, 1)
            for k in range(2):
                for s in range(2):
                    pool.wait_ge(nodes[k].y_stored[s], 16 * BLOCKS_OF[s])
                over_edges(pool, gather_edges(k))
                gather_ends(k)

        @block.tensor
        def _(pe):
            def turn(k, a, s):
                m = nodes[k]
                wait(pe, m.feat_ready, a + 1)
                wait(pe, m.turn_copied, a - 1)
                for t in range(TPB):
                    mm = pe.transpose(ps_turn[s][0:D, t * P:(t + 1) * P], feat[s][:, t, :], ident[:])
                mm.then_inc(m.turned, 1)

            def project(k, a, s):
                m = nodes[k]
                wait(pe, m.turn_copied, a + 1)
                wait(pe, m.y_copied, a - 1)
                wait(pe, m.root_copied, a - 1)
                for t in range(TPB):
                    mm = pe.matmul(ps_node[s][:, t // 2, t % 2, :], feat_t[s][:, t * P:(t + 1) * P],
                                   w_node[k][:], start=True, stop=True)
                mm.then_inc(m.projected, 1)

            def turn_and_project(k):
                def step(a, s, u):
                    turn(k, a + 1, 1 - s)
                    project(k, a, s)
                turn(k, 0, 0)
                over_group(pe, step, 0, NBLK - 2)
                step(NBLK - 2, 1, None)
                project(k, NBLK - 1, 0)

            def form_messages(k):
                m = edges[k]

                def step(i, p, tiles):
                    for b, count in enumerate(tiles):
                        n, w, s = i * 4 + 2 * p + b, count * P, 2 * p + b
                        if b == 0:
                            wait(pe, m.ea_loaded[p], i * 32 + 32)
                        wait(pe, m.mask_copied, n - 1)
                        pe.matmul(ps_mask[b][0:D, 0:w], big_row[:], mask_row[p][:, b * BLOCK:b * BLOCK + w],
                                  start=True, stop=True).then_inc(m.mask_spread, 1)
                        wait(pe, m.scanned, n - 1)
                        wait(pe, m.gathered[s], i * (16 * TPB) + 16 * count)
                        for t in range(count):
                            pe.matmul(ps_msg[b][0:D, t * P:(t + 1) * P], rows[s][:, t, :], ident[:],
                                      is_transpose=True, start=(t == 0), stop=False)
                        pe.matmul(ps_msg[b][0:D, 0:w], w_edge[k][s * DE:(s + 1) * DE, :],
                                  ea_sb[s * DE:(s + 1) * DE, 0:w], start=False, stop=True).then_inc(m.messages, 1)
                    if k == 0:
                        for b, count in enumerate(tiles):
                            n = i * 4 + 2 * p + b
                            wait(pe, m.hot_ready, n + 1)
                            for t in range(count):
                                first = isinstance(n, int) and n == 0 and t == 0
                                last = isinstance(n, int) and n == EBLK - 1 and t == count - 1
                                mm = pe.matmul(ps_count[:, 0:NCOL], hot_p[b][:, t, :], hot_c[b][:, t, :],
                                               start=first, stop=last, skip_group_check=True)
                            mm.then_inc(m.hot_used, 1)
                    for b, count in enumerate(tiles):
                        n = i * 4 + 2 * p + b
                        wait(pe, m.scanned, n + 1)
                        wait(pe, m.back_copied, n - 1)
                        for t in range(count):
                            mm = pe.transpose(ps_back[b][:, t * D:(t + 1) * D], run[b][:, t * P:(t + 1) * P],
                                              ident[0:D, 0:D])
                        mm.then_inc(m.back, 1)
                return step

            pe.wait_ge(s_const, 7)
            pe.wait_ge(s_iota, POOL_CONSTANTS)
            for k in range(2):
                pe.wait_ge(s_weights[k], 16 * 3)
                turn_and_project(k)
                pe.wait_ge(s_w_edge[k], 16 * 4)
                pe.wait_ge(nodes[k].y_copied, NBLK)
                pe.wait_ge(nodes[k].root_copied, NBLK)
                over_edges(pe, form_messages(k))
                if k == 0:
                    pe.wait_ge(s_deg, 2)
                    pe.matmul(ps_iota[:, 0:NBLK], below[:], deg_sum[:], start=True, stop=True)
                    pe.matmul(ps_iota[:, P:P + NBLK], ones[:], deg_sum[:], start=True,
                              stop=True).then_inc(s_deg_sums, 1)

        @block.scalar
        def _(act):
            def copy_turned(k, a, s):
                m = nodes[k]
                wait(act, m.turned, a + 1)
                wait(act, m.projected, a - 1)
                act.activation(feat_t[s][0:D, :], ps_turn[s][0:D, :], ACT.Relu if k == 0 else ACT.Copy
                               ).then_inc(m.turn_copied, 1)

            def copy_projected(k, a, s, u):
                m = nodes[k]
                wait(act, m.projected, a + 1)
                wait(act, m.y_stored[s], u * 16)
                act.activation(y_sb[s][:].rearrange("p (h t) d -> p h t d", h=2), ps_node[s][:, :, :, 0:D],
                               ACT.Copy).then_inc(m.y_copied, 1)
                act.activation(columns(root, a).rearrange("p (h t) d -> p h t d", h=2),
                               ps_node[s][:, :, :, D:2 * D], ACT.Copy).then_inc(m.root_copied, 1)

            def copy_nodes(k):
                def step(a, s, u):
                    copy_turned(k, a + 1, 1 - s)
                    copy_projected(k, a, s, u)
                copy_turned(k, 0, 0)
                over_group(act, step, 0, NBLK - 2)
                step(NBLK - 2, 1, (NBLK - 2) // 2)
                copy_projected(k, NBLK - 1, 0, (NBLK - 1) // 2)

            def move_edges(k):
                m = edges[k]

                def step(i, p, tiles):
                    for b, count in enumerate(tiles):
                        n, w = i * 4 + 2 * p + b, count * P
                        wait(act, m.mask_spread, n + 1)
                        wait(act, m.scanned, n - 1)
                        act.activation(mask_all[b][:, 0:w], ps_mask[b][0:D, 0:w], ACT.Copy
                                       ).then_inc(m.mask_copied, 1)
                    wait(act, m.run_stored[p], i * 16)
                    for b, count in enumerate(tiles):
                        n = i * 4 + 2 * p + b
                        wait(act, m.back, n + 1)
                        act.activation(run_rows[p][:, b * TPB:b * TPB + count, :],
                                       ps_back[b][:, 0:count * D].rearrange("p (t d) -> p t d", d=D),
                                       ACT.Copy).then_inc(m.back_copied, 1)
                    wait(act, m.back_copied, i * 4 + 2 * p + len(tiles))
                    act.dma_start(run_v[bass.ds(i * 2 + p, 1)].rearrange("o p f -> (o p) f"),
                                  run_rows[p][:].rearrange("p t d -> p (t d)")).then_inc(m.run_stored[p], 16)
                return step

            act.wait_ge(s_iota, POOL_CONSTANTS)
            act.activation(std[:, 0:1], eps[:], ACT.Sqrt).then_inc(s_std, 1)
            for g in range(len(GROUP)):
                cols = columns_of(g)
                act.wait_ge(s_centered, g + 1)
                wait(act, s_square_sum, g - 1)
                act.activation(square[g % 2][:, 0:cols.stop - cols.start, :], root[:, cols, :], ACT.Square
                               ).then_inc(s_squared, 1)
            act.wait_ge(s_square_sum, len(GROUP))
            act.wait_ge(s_std, 1)
            act.activation(std[:], square_sum[:], ACT.Sqrt, bias=eps[:, 0:1], scale=1.0 / D).then_inc(s_std, 1)
            copy_nodes(0)
            over_edges(act, move_edges(0))
            copy_nodes(1)
            over_edges(act, move_edges(1))

        @block.vector
        def _(dve):
            def chain(sm):
                done = [0]

                def step(ins):
                    done[0] += 1
                    ins.then_inc(sm, 1)
                    dve.wait_ge(sm, done[0])
                return step

            def normalise(a, s, u):
                wait(dve, nodes[0].turned, a - 1)
                dve.tensor_tensor(feat[s][:], columns(root, a),
                                  columns(rstd, a).unsqueeze(2).to_broadcast([P, TPB, D]), ALU.mult
                                  ).then_inc(nodes[0].feat_ready, 1)

            def scan(k):
                m = edges[k]

                def step(i, p, tiles):
                    for b, count in enumerate(tiles):
                        n, w = i * 4 + 2 * p + b, count * P
                        if k == 0:
                            wait(dve, m.hot_used, n - 1)
                            for hot, of, size in ((hot_p, dst_p, P), (hot_c, dst_c, NCOL)):
                                shape = [P, count, size]
                                ins = dve.tensor_tensor(
                                    hot[b][:, 0:count, :],
                                    ps_iota[:, 0:size].unsqueeze(1).to_broadcast(shape),
                                    of[:, bass.ds(n * TPB, count)].unsqueeze(2).to_broadcast(shape), ALU.is_equal)
                            ins.then_inc(m.hot_ready, 1)
                        wait(dve, m.messages, n + 1)
                        wait(dve, m.mask_copied, n + 1)
                        wait(dve, m.back, n - 1)
                        wait(dve, m.scanned, n)
                        first = isinstance(n, int) and n == 0
                        dve.tensor_tensor_scan(run[b][:, 0:w], mask_all[b][:, 0:w], ps_msg[b][0:D, 0:w],
                                               0.0 if first else run[1 - b][:, BLOCK - 1:BLOCK],
                                               ALU.min, ALU.max).then_inc(m.scanned, 1)
                return step

            def find_ends():
                link = chain(s_deg)
                c_all = ps_count[:, 0:NCOL]
                link(dve.tensor_copy(deg[:], c_all))
                link(dve.tensor_reduce(deg_sum[:], c_all.rearrange("p (a t) -> p a t", t=TPB), AX.X, ALU.add))
                dve.wait_ge(s_deg_sums, 1)
                total = ps_iota[:, P:P + NBLK]
                link(dve.tensor_tensor_scan(through[:], ones[:, 0:NBLK], total, 0.0, ALU.mult, ALU.add))
                link(dve.tensor_tensor(through[:], through[:], total, ALU.subtract))
                link(dve.tensor_tensor(before[:], through[:], ps_iota[:, 0:NBLK], ALU.add))
                deg_v = deg[:].rearrange("p (a t) -> p a t", t=TPB)
                upto_v = upto[:].rearrange("p (a t) -> p a t", t=TPB)
                for t in range(TPB):
                    link(dve.tensor_tensor(upto_v[:, :, t], before[:] if t == 0 else upto_v[:, :, t - 1],
                                           deg_v[:, :, t], ALU.add))
                link(dve.tensor_scalar(end_e[:], upto[:], -1.0, 0.0, ALU.add, ALU.max))
                link(dve.tensor_scalar(has_edge[:], deg[:], 1.0, None, ALU.min))
                link(dve.tensor_scalar(end_x[:], end_e[:], P - 1, 3, ALU.bitwise_and, ALU.logical_shift_left))
                link(dve.tensor_scalar(end_y[:], end_e[:], 7, 7, ALU.logical_shift_right, ALU.bitwise_and))
                link(dve.tensor_scalar(end_e[:], end_e[:], 10, 10, ALU.logical_shift_right, ALU.logical_shift_left))
                link(dve.tensor_tensor(end_x[:], end_x[:], end_y[:], ALU.bitwise_or))
                link(dve.tensor_tensor(end_row[:], end_x[:], end_e[:], ALU.bitwise_or))

            def finish(k):
                m, steps = edges[k], 2 + k

                def step(a, s, u):
                    wait(dve, m.end_gathered[s], u * (16 * TPB) + 16 * TPB)
                    wait(dve, nodes[1].feat_ready if k == 0 else s_fin, a)
                    shape = [P, TPB, D]
                    dve.tensor_tensor(work[:], agg[s][:], columns(has_edge, a).unsqueeze(2).to_broadcast(shape),
                                      ALU.mult).then_inc(m.node_steps, 1)
                    wait(dve, m.node_steps, a * steps + 1)
                    dve.tensor_tensor(work[:], work[:], columns(root, a), ALU.add).then_inc(m.node_steps, 1)
                    wait(dve, m.node_steps, a * steps + 2)
                    if k == 0:
                        wait(dve, nodes[1].turned, a - 1)
                    ins = dve.scalar_tensor_tensor(out=feat[s][:], in0=work[:], scalar=SLOPE, in1=work[:],
                                                   op0=ALU.mult, op1=ALU.max)
                    if k == 0:
                        ins.then_inc(nodes[1].feat_ready, 1)
                    else:
                        ins.then_inc(m.node_steps, 1)
                        wait(dve, m.node_steps, a * steps + 3)
                        wait(dve, s_out[s], u * 16)
                        dve.tensor_tensor(y_sb[s][:], feat[s][:], columns(x_sb, a), ALU.add).then_inc(s_fin, 1)
                return step

            for s in range(2):
                dve.memset(feat_t[s][D:D + 1, :], 1.0).then_inc(s_const, 1)
                dve.memset(w_node[s][D:D + 1, 0:D], 0.0).then_inc(s_const, 1)
            dve.wait_ge(s_iota, POOL_CONSTANTS)
            dve.tensor_scalar(ident[:], iota_row[:], iota_part[:, 0:1], None, ALU.is_equal).then_inc(s_const, 1)
            dve.tensor_scalar(below[:], iota_row[:], iota_part[:, 0:1], None, ALU.is_gt).then_inc(s_const, 1)
            dve.tensor_copy(ps_iota[:, 0:P], iota_row[:]).then_inc(s_const, 1)

            def means(g):
                cols = columns_of(g)
                dve.wait_ge(s_x[g], 16)
                dve.tensor_reduce(mean[:, cols], x_sb[:, cols, :], AX.X, ALU.add).then_inc(s_sum, 1)
                dve.wait_ge(s_sum, g + 1)
                dve.tensor_scalar(mean[:, cols], mean[:, cols], 1.0 / D, None, ALU.mult).then_inc(s_mean, 1)

            def add_squares(g):
                cols = columns_of(g)
                dve.wait_ge(s_squared, g + 1)
                dve.tensor_reduce(square_sum[:, cols], square[g % 2][:, 0:cols.stop - cols.start, :], AX.X, ALU.add
                                  ).then_inc(s_square_sum, 1)

            def make_mask():
                dve.wait_ge(s_dst_runs, 32)
                dve.tensor_tensor(mask_sb[:], dst_b[:], dst_a[:], ALU.is_equal).then_inc(s_mask, 1)
                dve.wait_ge(s_mask, 1)
                dve.tensor_scalar(mask_sb[:], mask_sb[:], 2.0, -1.0, ALU.mult, ALU.add).then_inc(s_mask, 1)

            split_link = chain(s_split)

            def split_partition():
                dve.wait_ge(s_dst_tiles, 16)
                dve.wait_ge(s_mask, 2)
                split_link(dve.tensor_scalar(dst_a[:], dst_i[:], 2, P - 1, ALU.logical_shift_right, ALU.bitwise_and))
                split_link(dve.tensor_copy(dst_p[:], dst_a[:]))

            def split_column():
                split_link(dve.tensor_scalar(dst_b[:], dst_i[:], 9, 2, ALU.logical_shift_right, ALU.logical_shift_left))
                split_link(dve.tensor_scalar(dst_a[:], dst_i[:], TPB - 1, None, ALU.bitwise_and))
                split_link(dve.tensor_tensor(dst_c[:], dst_a[:], dst_b[:], ALU.add))

            for g in range(len(GROUP) + LAG):
                if g < len(GROUP):
                    means(g)
                if g >= LAG:
                    add_squares(g - LAG)
            dve.wait_ge(s_std, 2)
            dve.reciprocal(rstd[:], std[:]).then_inc(s_rstd, 1)
            dve.wait_ge(s_rstd, 1)
            over_group(dve, normalise, 0, 7)
            make_mask()
            over_group(dve, normalise, 7, 13)
            split_partition()
            over_group(dve, normalise, 13, 19)
            split_column()
            over_group(dve, normalise, 19, NBLK)

            over_edges(dve, scan(0))
            dve.wait_ge(edges[0].hot_used, EBLK)
            find_ends()
            over_nodes(dve, finish(0))
            over_edges(dve, scan(1))
            over_nodes(dve, finish(1))


def kernel(**inputs):
    import concourse.bacc as bacc
    from concourse.bass_utils import run_bass_kernel_spmd

    a = {n: np.ascontiguousarray(v) for n, v in inputs.items()}
    x, src, dst, ea = a["x"], a["src"], a["dst"], a["edge_attr_32"]
    N, D = x.shape
    E, DE = ea.shape
    nblk, eblk = cdiv(N, BLOCK), cdiv(E, BLOCK)
    npair = cdiv(eblk, 2)

    x_pad = np.zeros((nblk * BLOCK, D), x.dtype)
    x_pad[:N] = x
    src_pad = np.zeros(npair * PAIR, src.dtype)
    src_pad[:E] = src
    dst_run = np.full(1 + eblk * BLOCK, N, dst.dtype)
    dst_run[0] = -1
    dst_run[1:E + 1] = dst
    ea_pad = np.zeros((eblk * BLOCK, DE), ea.dtype)
    ea_pad[:E] = ea
    arrays = {
        "x_pad": x_pad,
        "src_tiles": np.ascontiguousarray(src_pad.reshape(npair, 2 * TPB, P).transpose(0, 2, 1)),
        "dst_tiles": np.ascontiguousarray(dst_run[1:].reshape(eblk * TPB, P).T),
        "dst_run": dst_run,
        "edge_attr_t": np.ascontiguousarray(ea_pad.reshape(eblk, BLOCK, DE).transpose(0, 2, 1)),
    }
    names = [[f"L0_gnn_{w}" for w in (f"W{k}_msg", f"W{k}_edge", f"W{k}_root", f"b{k}")] for k in (1, 2)]
    arrays |= {n: a[n] for layer in names for n in layer}

    nc = bacc.Bacc("TRN2", target_bir_lowering=False, num_devices=1)
    aps = {n: nc.dram_tensor(n, v.shape, mybir.dt.from_np(v.dtype), kind="ExternalInput").ap()
           for n, v in arrays.items()}
    out = nc.dram_tensor("out", (N, D), F32, kind="ExternalOutput").ap()
    build(nc, aps["x_pad"], aps["src_tiles"], aps["dst_tiles"], aps["dst_run"], aps["edge_attr_t"],
          [[aps[n] for n in layer] for layer in names], out, N, E)
    r = run_bass_kernel_spmd(nc, [{n: v for n, v in arrays.items()}], core_ids=[0])
    return r.results[0]["out"]
```

```python
from contextlib import ExitStack

import numpy as np

import concourse.bass as bass
from concourse import mybir

ALU = mybir.AluOpType
ACT = mybir.ActivationFunctionType
AX = mybir.AxisListType
F32 = mybir.dt.float32
BF16 = mybir.dt.bfloat16
I32 = mybir.dt.int32

P = 128
TPB = 4
BLOCK = P * TPB
PAIR = 2 * BLOCK
EPS = 1e-5
SLOPE = 0.01
BIG = 3.3895313892515355e38


def cdiv(a, b):
    return -(-a // b)


def wait(eng, sem, value):
    if isinstance(value, int) and value <= 0:
        return
    eng.wait_ge(sem, value)


def build(nc, x, src_t, dst_t, dst_run, ea_t, weights, out, N, E):
    D = x.shape[1]
    DE = ea_t.shape[1]
    NBLK = x.shape[0] // BLOCK
    NCOL = NBLK * TPB
    EBLK = ea_t.shape[0]
    ECOL = EBLK * TPB
    ITERS = (EBLK - 3) // 4
    LAST_TILES = cdiv(E - (EBLK - 1) * BLOCK, P)
    assert EBLK == 4 * ITERS + 3 and NBLK % 4 == 1 and D == 96 and DE == 32 and NCOL <= P
    NPAIR = cdiv(EBLK, 2)
    ROUNDS = NBLK // 4
    NODE_PAIRS = cdiv(NBLK, 2)
    LAST_P = (N - (NBLK - 1) * BLOCK) // TPB
    assert N % TPB == 0

    y_table = nc.dram_tensor("y_table", (NBLK * BLOCK, D), F32, kind="Internal").ap()
    run_table = nc.dram_tensor("run_table", (NPAIR * PAIR, D), F32, kind="Internal").ap()
    mask_table = nc.dram_tensor("mask_table", (EBLK * BLOCK,), BF16, kind="Internal").ap()

    x_v = x.rearrange("(a p t) d -> p a (t d)", p=P, t=TPB)
    y_v = y_table.rearrange("(a p t) d -> p a (t d)", p=P, t=TPB)
    out_v = out[0:(NBLK - 1) * BLOCK].rearrange("(a p t) d -> a p (t d)", p=P, t=TPB)
    out_last = out[(NBLK - 1) * BLOCK:N].rearrange("(p t) d -> p (t d)", t=TPB)
    run_v = run_table.rearrange("(q p t) d -> q p (t d)", p=P, t=2 * TPB)
    mask_store = mask_table.rearrange("(p c) -> p c", p=P)
    mask_load = mask_table.rearrange("(o e) -> o e", o=1)
    ea_v = ea_t.rearrange("b f e -> (b f) e")

    with ExitStack() as ctx:
        def sb(name, shape, dt):
            return ctx.enter_context(nc.sbuf_tensor(name, shape, dt))

        def banks(name, n):
            return ctx.enter_context(nc.psum_tensor(name, [P, n, BLOCK], F32))

        def sem(name):
            return ctx.enter_context(nc.semaphore(name))

        x_sb = sb("x_sb", [P, NCOL, D], F32)
        root = sb("root", [P, NCOL, D], F32)
        has_edge = sb("has_edge", [P, NCOL], F32)
        end_row = sb("end_row", [P, NCOL], I32)
        ident = sb("ident", [P, P], F32)
        below = sb("below", [P, P], F32)
        ones = sb("ones", [P, P], F32)
        big_row = sb("big_row", [1, D], BF16)
        w_node = [sb(f"w_node{k}", [D + 1, 2 * D], F32) for k in range(2)]
        w_edge = [sb(f"w_edge{k}", [P, D], F32) for k in range(2)]
        dst_p = sb("dst_p", [P, ECOL], BF16)
        dst_c = sb("dst_c", [P, ECOL], BF16)
        dst_a = sb("dst_a", [P, ECOL], I32)
        dst_b = sb("dst_b", [P, ECOL], I32)
        dst_seq = sb("dst_seq", [P, ECOL + 1], I32)
        dst_i = sb("dst_i", [P, ECOL], I32)
        mask_sb = sb("mask_sb", [P, ECOL], BF16)
        iota_row = sb("iota_row", [P, P], F32)
        iota_part = sb("iota_part", [P, 1], F32)
        mean = sb("mean", [P, NCOL], F32)
        square_sum = sb("square_sum", [P, NCOL], F32)
        std = sb("std", [P, NCOL], F32)
        rstd = sb("rstd", [P, NCOL], F32)
        centered = [sb(f"centered{p}", [P, 2 * TPB, D], F32) for p in range(2)]
        square = [sb(f"square{p}", [P, 2 * TPB, D], F32) for p in range(2)]
        eps = sb("eps", [P, 1], F32)
        feat = [sb(f"feat{s}", [P, TPB, D], F32) for s in range(2)]
        norm = sb("norm", [P, TPB, D], F32)
        feat_t = [sb(f"feat_t{s}", [D + 1, BLOCK], F32) for s in range(2)]
        y_sb = [sb(f"y_sb{s}", [P, 2 * TPB, D], F32) for s in range(2)]
        agg = [sb(f"agg{s}", [P, TPB, D], F32) for s in range(2)]
        work = sb("work", [P, TPB, D], F32)
        idx = [sb(f"idx{p}", [P, 2 * TPB], I32) for p in range(2)]
        ea_sb = sb("ea_sb", [P, BLOCK], F32)
        mask_row = [sb(f"mask_row{p}", [1, PAIR], BF16) for p in range(2)]
        rows = [sb(f"rows{s}", [P, TPB, D], F32) for s in range(4)]
        mask_all = [sb(f"mask_all{b}", [D, BLOCK], BF16) for b in range(2)]
        run = [sb(f"run{b}", [D, BLOCK], F32) for b in range(2)]
        run_rows = [sb(f"run_rows{p}", [P, 2 * TPB, D], F32) for p in range(2)]
        hot_p = [sb(f"hot_p{b}", [P, TPB, P], BF16) for b in range(2)]
        hot_c = [sb(f"hot_c{b}", [P, TPB, NCOL], BF16) for b in range(2)]
        deg = sb("deg", [P, NCOL], F32)
        deg_sum = sb("deg_sum", [P, NBLK], F32)
        through = sb("through", [P, NBLK], F32)
        before = sb("before", [P, NBLK], F32)
        upto = sb("upto", [P, NCOL], F32)
        end_e = sb("end_e", [P, NCOL], I32)
        end_x = sb("end_x", [P, NCOL], I32)
        end_y = sb("end_y", [P, NCOL], I32)

        pair_a, pair_b, pair_c = (banks(n, 2) for n in ("pair_a", "pair_b", "pair_c"))
        ps_count = banks("ps_count", 1)[:, 0, :]
        ps_iota = banks("ps_iota", 1)[:, 0, :]
        ps_msg = ps_turn = [pair_a[:, b, :] for b in range(2)]
        ps_mask = [pair_b[:, b, :] for b in range(2)]
        ps_back = [pair_c[:, b, :] for b in range(2)]
        ps_y = [v[:, :, 0:4 * D] for v in (pair_b, pair_c)]
        ps_c1_t, ps_norm_t = ps_turn
        ps_root = [v[:, 0:TPB * D].rearrange("p (t d) -> p t d", d=D) for v in (ps_count, ps_iota)]
        ps_node = [v[:, :, 0:4 * D].rearrange("p h (t d) -> p h t d", t=2) for v in (pair_b, pair_c)]

        s_x = [sem(f"x_loaded{p}") for p in range(2)]
        s_weights = [sem(f"node_weights_loaded{k}") for k in range(2)]
        s_w_edge = [sem(f"edge_weights_loaded{k}") for k in range(2)]
        s_dst_runs = sem("dst_runs_loaded")
        s_dst_tiles = sem("dst_tiles_loaded")
        s_iota = sem("iota_made")
        s_const = sem("constants_made")
        s_mask = sem("mask_steps")
        s_mask_stored = sem("mask_stored")
        s_split = sem("dst_split_steps")
        s_sum = sem("sums_made")
        s_mean = sem("means_made")
        s_centered = sem("centered")
        s_squared = sem("squared")
        s_square_sum = sem("square_sums_made")
        s_table = sem("function_table_loaded")
        s_std = sem("std_made")
        s_rstd = sem("rstd_made")
        s_turned = sem("centered_turned")
        s_turn_copied = sem("centered_turn_copied")
        s_y_projected = sem("start_y_projected")
        s_y_scaled = sem("start_y_scaled")
        s_y_stored = [sem(f"start_y_stored{p}") for p in range(2)]
        s_norm_sub = sem("norm_centered")
        s_norm = sem("norm_made")
        s_norm_turned = sem("norm_turned")
        s_norm_t_copied = sem("norm_turn_copied")
        s_root1 = sem("layer1_root_made")
        s_feat = sem("c1_made")
        s_feat_turned = sem("c1_turned")
        s_feat_t_copied = sem("c1_turn_copied")
        s_projected = sem("c1_projected")
        s_y_copied = sem("y_copied")
        s_root_copied = sem("root_copied")
        s_y2_stored = [sem(f"y_stored{s}") for s in range(2)]
        s_deg = sem("degree_steps")
        s_deg_sums = sem("degree_sums_made")
        s_fin = sem("output_made")
        s_out = [sem(f"output_stored{s}") for s in range(2)]

        class Edges:
            def __init__(self, k):
                self.idx_loaded = [sem(f"idx_loaded{k}_{p}") for p in range(2)]
                self.ea_loaded = [sem(f"ea_loaded{k}_{p}") for p in range(2)]
                self.gathered = [sem(f"gathered{k}_{s}") for s in range(4)]
                self.mask_spread = sem(f"mask_spread{k}")
                self.mask_copied = sem(f"mask_copied{k}")
                self.messages = sem(f"messages{k}")
                self.hot_ready = sem(f"hot_ready{k}")
                self.hot_used = sem(f"hot_used{k}")
                self.scanned = sem(f"scanned{k}")
                self.back = sem(f"back{k}")
                self.back_copied = sem(f"back_copied{k}")
                self.run_stored = [sem(f"run_stored{k}_{p}") for p in range(2)]
                self.end_gathered = [sem(f"end_gathered{k}_{s}") for s in range(2)]
                self.node_steps = sem(f"node_steps{k}")

        POOL_CONSTANTS = 5
        CONSTANTS = 6
        DEGREE_STEPS = 16

        edges = [Edges(k) for k in range(2)]

        def over_nodes(eng, step, count=NBLK):
            for a in range(3):
                step(a, a % 2, a // 2)
            with eng.Fori(1, count // 2) as i:
                step(i * 2 + 1, 1, i)
                step(i * 2 + 2, 0, i + 1)

        def over_node_pairs(eng, step):
            for j in range(4):
                step(j // 2, j % 2, 2)
            with eng.Fori(2, ROUNDS) as i:
                for p in range(2):
                    step(i, p, 2)
            step(ROUNDS, 0, 1)

        def pair_columns(v, j, n=2):
            return v[:, bass.ds(j * (2 * TPB), n * TPB)]

        def over_edges(eng, step):
            for p in range(2):
                step(0, p, [TPB, TPB])
            with eng.Fori(1, ITERS) as i:
                for p in range(2):
                    step(i, p, [TPB, TPB])
            step(ITERS, 0, [TPB, TPB])
            step(ITERS, 1, [LAST_TILES])

        PAIRS_OF = [cdiv(NPAIR, 2), NPAIR // 2]
        BLOCKS_OF = [cdiv(NBLK, 2), NBLK // 2]

        def columns(v, a):
            return v[:, bass.ds(a * TPB, TPB)]

        def wait_y_stored(eng, k):
            for s in range(2):
                uses, stored = (NODE_PAIRS, s_y_stored) if k == 0 else (NBLK, s_y2_stored)
                eng.wait_ge(stored[s], 16 * ((uses + 1 - s) // 2))

        def load_node_weights(eng, k):
            w_msg, _, w_root, bias = weights[k]
            eng.dma_start(w_node[k][0:D, 0:D], w_msg).then_inc(s_weights[k], 16)
            eng.dma_start(w_node[k][0:D, D:2 * D], w_root).then_inc(s_weights[k], 16)
            eng.dma_start(w_node[k][D:D + 1, D:2 * D], bias.rearrange("(o d) -> o d", o=1)).then_inc(s_weights[k], 16)

        block = ctx.enter_context(nc.Block())

        @block.sync
        def _(sp):
            def load_x(i, p, n):
                wait(sp, s_x[p], i * 16)
                a = i * 4 + 2 * p
                sp.dma_start(x_sb[:, bass.ds(a * TPB, n * TPB), :].rearrange("p (a t) d -> p a (t d)", t=TPB),
                             x_v[:, bass.ds(a, n)]).then_inc(s_x[p], 16)

            def load_edge_weights(k):
                for r in range(4):
                    sp.dma_start(w_edge[k][r * DE:(r + 1) * DE, :], weights[k][1]).then_inc(s_w_edge[k], 16)

            def store_y(a, s, u):
                wait(sp, s_y_copied, a + 1)
                sp.dma_start(y_v[:, bass.ds(a, 1)].rearrange("p o f -> p (o f)"),
                             y_sb[s][:, 0:TPB].rearrange("p t d -> p (t d)")).then_inc(s_y2_stored[s], 16)

            def store_mask():
                sp.wait_ge(s_mask, 2)
                sp.dma_start(mask_store, mask_sb[:]).then_inc(s_mask_stored, 16)
                sp.wait_ge(s_mask_stored, 16)

            def load_edges(k):
                m = edges[k]

                def step(i, p, tiles):
                    q, n, w = i * 2 + p, i * 4 + 2 * p, len(tiles)
                    for b in range(2):
                        wait(sp, m.gathered[2 * p + b], i * (16 * TPB))
                    sp.dma_start(idx[p][:], src_t[bass.ds(q, 1)].rearrange("o p t -> (o p) t")
                                 ).then_inc(m.idx_loaded[p], 16)
                    wait(sp, m.messages, n - 2)
                    sp.dma_start(ea_sb[2 * p * DE:(2 * p + w) * DE, :],
                                 ea_v[bass.ds(n * DE, w * DE), :]).then_inc(m.ea_loaded[p], 16)
                    if k == 0 and isinstance(i, int) and i + p == 0:
                        store_mask()
                    sp.dma_start(mask_row[p][:, 0:w * BLOCK],
                                 mask_load[:, bass.ds(n * BLOCK, w * BLOCK)]).then_inc(m.ea_loaded[p], 16)
                return step

            def store_out(a, s, u):
                wait(sp, s_fin, a + 1)
                sp.dma_start(out_v[bass.ds(a, 1)].rearrange("o p f -> (o p) f"),
                             y_sb[s][:, 0:TPB].rearrange("p t d -> p (t d)")).then_inc(s_out[s], 16)

            over_node_pairs(sp, load_x)
            sp.dma_start(dst_seq[:], dst_run).then_inc(s_dst_runs, 16)
            load_edge_weights(0)
            over_edges(sp, load_edges(0))
            load_node_weights(sp, 1)
            load_edge_weights(1)
            over_nodes(sp, store_y)
            over_edges(sp, load_edges(1))
            over_nodes(sp, store_out, NBLK - 2)
            store_out(NBLK - 2, 1, NBLK // 2 - 1)
            sp.wait_ge(s_fin, NBLK)
            sp.dma_start(out_last, y_sb[0][0:LAST_P, 0:TPB].rearrange("p t d -> p (t d)")).then_inc(s_out[0], 16)
            for s in range(2):
                sp.wait_ge(s_out[s], 16 * BLOCKS_OF[s])

        @block.gpsimd
        def _(pool):
            def gather(dst, table, index):
                return pool.indirect_dma_start(out=dst, out_offset=None, in_=table,
                                               in_offset=bass.IndirectOffsetOnAxis(ap=index, axis=0))

            def gather_edges(k):
                m = edges[k]

                def step(i, p, tiles):
                    for b, count in enumerate(tiles):
                        s = 2 * p + b
                        if b == 0:
                            wait(pool, m.idx_loaded[p], i * 16 + 16)
                        wait(pool, m.messages, i * 4 + s - 3)
                        pool.nop(nofuse=True)
                        for t in range(count):
                            gather(rows[s][:, t, :], y_table, idx[p][:, t + TPB * b:t + TPB * b + 1]
                                   ).then_inc(m.gathered[s], 16)
                return step

            def gather_ends(k):
                m = edges[k]
                for p in range(2):
                    pool.wait_ge(m.run_stored[p], 16 * PAIRS_OF[p])
                pool.wait_ge(s_deg, DEGREE_STEPS)
                for a in range(NBLK):
                    wait(pool, m.node_steps, (2 + k) * (a - 2) + 1)
                    for t in range(TPB):
                        c = a * TPB + t
                        gather(agg[a % 2][:, t, :], run_table, end_row[:, c:c + 1]).then_inc(m.end_gathered[a % 2], 16)

            pool.iota(iota_row[:], [[1, P]], base=0, channel_multiplier=0,
                      allow_small_or_imprecise_dtypes=True).then_inc(s_iota, 1)
            pool.iota(iota_part[:], [[0, 1]], base=0, channel_multiplier=1,
                      allow_small_or_imprecise_dtypes=True).then_inc(s_iota, 1)
            pool.memset(ones[:], 1.0).then_inc(s_iota, 1)
            pool.memset(big_row[:], BIG).then_inc(s_iota, 1)
            pool.memset(eps[:], EPS).then_inc(s_iota, 1)

            def center(i, p, n):
                j, w = i * 2 + p, n * TPB
                wait(pool, s_mean, j + 1)
                wait(pool, s_squared, j - 1)
                wait(pool, s_turned, 2 * j - 2)
                pool.tensor_tensor(centered[p][:, 0:w, :], pair_columns(x_sb, j, n),
                                   pair_columns(mean, j, n).unsqueeze(2).to_broadcast([P, w, D]),
                                   ALU.subtract).then_inc(s_centered, 1)

            over_node_pairs(pool, center)
            for k in range(2):
                wait_y_stored(pool, k)
                over_edges(pool, gather_edges(k))
                gather_ends(k)

        @block.tensor
        def _(pe):
            def turn_start(i, p, n):
                j = i * 2 + p
                wait(pe, s_centered, j + 1)
                for b in range(n):
                    wait(pe, s_turn_copied, 2 * j + b - 1)
                    for t in range(TPB):
                        mm = pe.transpose(ps_turn[b][0:D, t * P:(t + 1) * P], centered[p][:, b * TPB + t, :], ident[:])
                    mm.then_inc(s_turned, 1)

            def project_start(j, p, n):
                wait(pe, s_y_scaled, j - 1)
                for b in range(n):
                    wait(pe, s_turn_copied, 2 * j + b + 1)
                    for t in range(TPB):
                        mm = pe.matmul(ps_y[p][:, b, t * D:(t + 1) * D], feat_t[b][0:D, t * P:(t + 1) * P],
                                       w_node[0][0:D, 0:D], start=True, stop=True)
                    mm.then_inc(s_y_projected, 1)

            def turn_and_project(i, p, n):
                turn_start(i, p, n)
                if not (isinstance(i, int) and i + p == 0):
                    project_start(i * 2 + p - 1, 1 - p, 2)

            def turn_norm(a):
                wait(pe, s_norm, a + 1)
                wait(pe, s_norm_t_copied, a)
                for t in range(TPB):
                    mm = pe.transpose(ps_norm_t[0:D, t * P:(t + 1) * P], norm[:, t, :], ident[:])
                mm.then_inc(s_norm_turned, 1)

            def project_root1(a, s):
                wait(pe, s_norm_t_copied, a + 1)
                wait(pe, edges[0].node_steps, 2 * a - 2)
                for t in range(TPB):
                    mm = pe.matmul(ps_root[s][:, t, :], feat_t[0][:, t * P:(t + 1) * P], w_node[0][:, D:2 * D],
                                   start=True, stop=True)
                mm.then_inc(s_root1, 1)

            def turn_c1(a, s):
                wait(pe, s_feat, a + 1)
                wait(pe, s_feat_t_copied, a)
                for t in range(TPB):
                    mm = pe.transpose(ps_c1_t[0:D, t * P:(t + 1) * P], feat[s][:, t, :], ident[:])
                mm.then_inc(s_feat_turned, 1)

            def project_c1(a, s):
                wait(pe, s_feat_t_copied, a + 1)
                wait(pe, s_y_copied, a - 1)
                wait(pe, s_root_copied, a - 1)
                for t in range(TPB):
                    mm = pe.matmul(ps_node[s][:, t // 2, t % 2, :], feat_t[1][:, t * P:(t + 1) * P],
                                   w_node[1][:], start=True, stop=True)
                mm.then_inc(s_projected, 1)

            def nodes_between():
                def step(a, s, u):
                    turn_c1(a, s)
                    turn_norm(a + 2)
                    project_c1(a, s)
                    project_root1(a + 2, s)
                for a in range(2):
                    turn_norm(a)
                    project_root1(a, a)
                over_nodes(pe, step, NBLK - 2)
                for a in (NBLK - 2, NBLK - 1):
                    turn_c1(a, a % 2)
                    project_c1(a, a % 2)

            def form_messages(k):
                m = edges[k]

                def step(i, p, tiles):
                    for b, count in enumerate(tiles):
                        n, w, s = i * 4 + 2 * p + b, count * P, 2 * p + b
                        if b == 0:
                            wait(pe, m.ea_loaded[p], i * 32 + 32)
                        wait(pe, m.mask_copied, n - 1)
                        pe.matmul(ps_mask[b][0:D, 0:w], big_row[:], mask_row[p][:, b * BLOCK:b * BLOCK + w],
                                  start=True, stop=True).then_inc(m.mask_spread, 1)
                        wait(pe, m.scanned, n - 1)
                        wait(pe, m.gathered[s], i * (16 * TPB) + 16 * count)
                        for t in range(count):
                            pe.matmul(ps_msg[b][0:D, t * P:(t + 1) * P], rows[s][:, t, :], ident[:],
                                      is_transpose=True, start=(t == 0), stop=False)
                        pe.matmul(ps_msg[b][0:D, 0:w], w_edge[k][s * DE:(s + 1) * DE, :],
                                  ea_sb[s * DE:(s + 1) * DE, 0:w], start=False, stop=True).then_inc(m.messages, 1)
                    if k == 0:
                        for b, count in enumerate(tiles):
                            n = i * 4 + 2 * p + b
                            wait(pe, m.hot_ready, n + 1)
                            for t in range(count):
                                first = isinstance(n, int) and n == 0 and t == 0
                                last = isinstance(n, int) and n == EBLK - 1 and t == count - 1
                                mm = pe.matmul(ps_count[:, 0:NCOL], hot_p[b][:, t, :], hot_c[b][:, t, :],
                                               start=first, stop=last, skip_group_check=True)
                            mm.then_inc(m.hot_used, 1)
                    for b, count in enumerate(tiles):
                        n = i * 4 + 2 * p + b
                        wait(pe, m.scanned, n + 1)
                        wait(pe, m.back_copied, n - 1)
                        for t in range(count):
                            mm = pe.transpose(ps_back[b][:, t * D:(t + 1) * D], run[b][:, t * P:(t + 1) * P],
                                              ident[0:D, 0:D])
                        mm.then_inc(m.back, 1)
                return step

            pe.wait_ge(s_const, CONSTANTS)
            pe.wait_ge(s_iota, POOL_CONSTANTS)
            pe.wait_ge(s_weights[0], 16 * 3)
            over_node_pairs(pe, turn_and_project)
            project_start(NODE_PAIRS - 1, 0, 1)

            pe.wait_ge(s_w_edge[0], 16 * 4)
            pe.wait_ge(s_turn_copied, NBLK)
            pe.wait_ge(s_y_scaled, NODE_PAIRS)
            over_edges(pe, form_messages(0))
            pe.wait_ge(s_deg, 2)
            pe.matmul(ps_iota[:, 0:NBLK], below[:], deg_sum[:], start=True, stop=True)
            pe.matmul(ps_iota[:, P:P + NBLK], ones[:], deg_sum[:], start=True, stop=True).then_inc(s_deg_sums, 1)

            pe.wait_ge(s_weights[1], 16 * 3)
            pe.wait_ge(s_deg, DEGREE_STEPS)
            pe.wait_ge(edges[0].mask_copied, EBLK)
            pe.wait_ge(edges[0].back_copied, EBLK)
            nodes_between()

            pe.wait_ge(s_w_edge[1], 16 * 4)
            pe.wait_ge(s_y_copied, NBLK)
            pe.wait_ge(s_root_copied, NBLK)
            over_edges(pe, form_messages(1))

        @block.scalar
        def _(act):
            def start(i, p, n):
                j, w = i * 2 + p, n * TPB
                if not (isinstance(i, int) and i + p == 0):
                    make_std(j - 1, 2)
                wait(act, s_centered, j + 1)
                wait(act, s_square_sum, j - 1)
                act.activation(square[p][:, 0:w, :], centered[p][:, 0:w, :], ACT.Square).then_inc(s_squared, 1)
                for b in range(n):
                    wait(act, s_turned, 2 * j + b + 1)
                    wait(act, s_y_projected, 2 * j + b - 1)
                    act.activation(feat_t[b][0:D, :], ps_turn[b][0:D, :], ACT.Relu).then_inc(s_turn_copied, 1)
                if not (isinstance(i, int) and i == 0):
                    store_scaled(j - 2, p, 2)

            def make_std(j, n):
                wait(act, s_square_sum, j + 1)
                act.activation(pair_columns(std, j, n), pair_columns(square_sum, j, n), ACT.Sqrt,
                               bias=eps[:, 0:1], scale=1.0 / D).then_inc(s_std, 1)

            def store_scaled(j, p, n):
                wait(act, s_y_scaled, j + 1)
                act.dma_start(y_v[:, bass.ds(j * 2, n)],
                              y_sb[p][:, 0:n * TPB].rearrange("p (a t) d -> p a (t d)", t=TPB)
                              ).then_inc(s_y_stored[p], 16)

            def copy_norm(a):
                wait(act, s_norm_turned, a + 1)
                wait(act, s_root1, a)
                act.activation(feat_t[0][0:D, :], ps_norm_t[0:D, :], ACT.Relu).then_inc(s_norm_t_copied, 1)

            def copy_turned(a):
                wait(act, s_feat_turned, a + 1)
                wait(act, s_projected, a)
                act.activation(feat_t[1][0:D, :], ps_c1_t[0:D, :], ACT.Copy).then_inc(s_feat_t_copied, 1)

            def copy_projected(a, s, u):
                wait(act, s_projected, a + 1)
                wait(act, s_y2_stored[s], u * 16)
                act.activation(y_sb[s][:, 0:TPB].rearrange("p (h t) d -> p h t d", h=2), ps_node[s][:, :, :, 0:D],
                               ACT.Copy).then_inc(s_y_copied, 1)
                act.activation(columns(root, a).rearrange("p (h t) d -> p h t d", h=2),
                               ps_node[s][:, :, :, D:2 * D], ACT.Copy).then_inc(s_root_copied, 1)

            def copy_nodes():
                def step(a, s, u):
                    copy_turned(a)
                    copy_norm(a + 2)
                    copy_projected(a, s, u)
                for a in range(2):
                    copy_norm(a)
                over_nodes(act, step, NBLK - 2)
                for a in (NBLK - 2, NBLK - 1):
                    copy_turned(a)
                    copy_projected(a, a % 2, a // 2)

            def move_edges(k):
                m = edges[k]

                def step(i, p, tiles):
                    for b, count in enumerate(tiles):
                        n, w = i * 4 + 2 * p + b, count * P
                        wait(act, m.mask_spread, n + 1)
                        wait(act, m.scanned, n - 1)
                        act.activation(mask_all[b][:, 0:w], ps_mask[b][0:D, 0:w], ACT.Copy
                                       ).then_inc(m.mask_copied, 1)
                    wait(act, m.run_stored[p], i * 16)
                    for b, count in enumerate(tiles):
                        n = i * 4 + 2 * p + b
                        wait(act, m.back, n + 1)
                        act.activation(run_rows[p][:, b * TPB:b * TPB + count, :],
                                       ps_back[b][:, 0:count * D].rearrange("p (t d) -> p t d", d=D),
                                       ACT.Copy).then_inc(m.back_copied, 1)
                    wait(act, m.back_copied, i * 4 + 2 * p + len(tiles))
                    act.dma_start(run_v[bass.ds(i * 2 + p, 1)].rearrange("o p f -> (o p) f"),
                                  run_rows[p][:].rearrange("p t d -> p (t d)")).then_inc(m.run_stored[p], 16)
                return step

            load_node_weights(act, 0)
            act.wait_ge(s_iota, POOL_CONSTANTS)
            act.activation(std[:, 0:1], eps[:], ACT.Sqrt).then_inc(s_table, 1)
            act.wait_ge(s_table, 1)
            over_node_pairs(act, start)
            make_std(NODE_PAIRS - 1, 1)
            store_scaled(NODE_PAIRS - 2, 1, 2)
            store_scaled(NODE_PAIRS - 1, 0, 1)
            act.dma_start(dst_i[:], dst_t).then_inc(s_dst_tiles, 16)
            over_edges(act, move_edges(0))
            copy_nodes()
            over_edges(act, move_edges(1))

        @block.vector
        def _(dve):
            def chain(sm):
                done = [0]

                def step(ins):
                    done[0] += 1
                    ins.then_inc(sm, 1)
                    dve.wait_ge(sm, done[0])
                return step

            def reduce_pair(i, p, n):
                j = i * 2 + p
                peeled = isinstance(i, int)
                wait(dve, s_x[p], i * 16 + 16)
                dve.tensor_reduce(pair_columns(mean, j, n), pair_columns(x_sb, j, n), AX.X, ALU.add
                                  ).then_inc(s_sum, 1)
                wait(dve, s_sum, j + 1)
                dve.tensor_scalar(pair_columns(mean, j, n), pair_columns(mean, j, n), 1.0 / D, None, ALU.mult
                                  ).then_inc(s_mean, 1)
                if not (peeled and i == 0):
                    invert_std(j - 2, 2)
                if not (peeled and i + p == 0):
                    add_squares(j - 1, 1 - p, 2)
                if not (peeled and i == 0):
                    scale_y(j - 2, p, 2)

            def add_squares(j, p, n):
                wait(dve, s_squared, j + 1)
                dve.tensor_reduce(pair_columns(square_sum, j, n), square[p][:, 0:n * TPB, :], AX.X, ALU.add
                                  ).then_inc(s_square_sum, 1)

            def invert_std(j, n):
                wait(dve, s_std, j + 1)
                dve.reciprocal(pair_columns(rstd, j, n), pair_columns(std, j, n)).then_inc(s_rstd, 1)

            def scale_y(j, p, n):
                wait(dve, s_rstd, j + 1)
                wait(dve, s_y_projected, 2 * j + n)
                wait(dve, s_y_stored[p], (j - p) * (16 // 2))
                dve.tensor_tensor(y_sb[p][:, 0:n * TPB].rearrange("p (a t) d -> p a t d", t=TPB),
                                  ps_y[p][:, 0:n, :].rearrange("p a (t d) -> p a t d", d=D),
                                  pair_columns(rstd, j, n).rearrange("p (a t) -> p a t", t=TPB).unsqueeze(3)
                                  .to_broadcast([P, n, TPB, D]), ALU.mult).then_inc(s_y_scaled, 1)

            def make_norm(a):
                shape = [P, TPB, D]
                wait(dve, s_norm_turned, a)
                dve.tensor_tensor(norm[:], columns(x_sb, a), columns(mean, a).unsqueeze(2).to_broadcast(shape),
                                  ALU.subtract).then_inc(s_norm_sub, 1)
                wait(dve, s_norm_sub, a + 1)
                dve.tensor_tensor(norm[:], norm[:], columns(rstd, a).unsqueeze(2).to_broadcast(shape), ALU.mult
                                  ).then_inc(s_norm, 1)

            def scan(k):
                m = edges[k]

                def step(i, p, tiles):
                    for b, count in enumerate(tiles):
                        n, w = i * 4 + 2 * p + b, count * P
                        if k == 0:
                            wait(dve, m.hot_used, n - 1)
                            for hot, of, size in ((hot_p, dst_p, P), (hot_c, dst_c, NCOL)):
                                shape = [P, count, size]
                                ins = dve.tensor_tensor(
                                    hot[b][:, 0:count, :],
                                    ps_iota[:, 0:size].unsqueeze(1).to_broadcast(shape),
                                    of[:, bass.ds(n * TPB, count)].unsqueeze(2).to_broadcast(shape), ALU.is_equal)
                            ins.then_inc(m.hot_ready, 1)
                        wait(dve, m.messages, n + 1)
                        wait(dve, m.mask_copied, n + 1)
                        wait(dve, m.back, n - 1)
                        wait(dve, m.scanned, n)
                        first = isinstance(n, int) and n == 0
                        dve.tensor_tensor_scan(run[b][:, 0:w], mask_all[b][:, 0:w], ps_msg[b][0:D, 0:w],
                                               0.0 if first else run[1 - b][:, BLOCK - 1:BLOCK],
                                               ALU.min, ALU.max).then_inc(m.scanned, 1)
                return step

            def find_ends():
                link = chain(s_deg)
                c_all = ps_count[:, 0:NCOL]
                link(dve.tensor_copy(deg[:], c_all))
                link(dve.tensor_reduce(deg_sum[:], c_all.rearrange("p (a t) -> p a t", t=TPB), AX.X, ALU.add))
                dve.wait_ge(s_deg_sums, 1)
                total = ps_iota[:, P:P + NBLK]
                link(dve.tensor_tensor_scan(through[:], ones[:, 0:NBLK], total, 0.0, ALU.mult, ALU.add))
                link(dve.tensor_tensor(through[:], through[:], total, ALU.subtract))
                link(dve.tensor_tensor(before[:], through[:], ps_iota[:, 0:NBLK], ALU.add))
                deg_v = deg[:].rearrange("p (a t) -> p a t", t=TPB)
                upto_v = upto[:].rearrange("p (a t) -> p a t", t=TPB)
                for t in range(TPB):
                    link(dve.tensor_tensor(upto_v[:, :, t], before[:] if t == 0 else upto_v[:, :, t - 1],
                                           deg_v[:, :, t], ALU.add))
                link(dve.tensor_scalar(end_e[:], upto[:], -1.0, 0.0, ALU.add, ALU.max))
                link(dve.tensor_scalar(has_edge[:], deg[:], 1.0, None, ALU.min))
                link(dve.tensor_scalar(end_x[:], end_e[:], P - 1, 3, ALU.bitwise_and, ALU.logical_shift_left))
                link(dve.tensor_scalar(end_y[:], end_e[:], 7, 7, ALU.logical_shift_right, ALU.bitwise_and))
                link(dve.tensor_scalar(end_e[:], end_e[:], 10, 10, ALU.logical_shift_right, ALU.logical_shift_left))
                link(dve.tensor_tensor(end_x[:], end_x[:], end_y[:], ALU.bitwise_or))
                link(dve.tensor_tensor(end_row[:], end_x[:], end_e[:], ALU.bitwise_or))

            def finish(k):
                m, steps = edges[k], 2 + k

                def step(a, s, u):
                    wait(dve, m.end_gathered[s], u * (16 * TPB) + 16 * TPB)
                    wait(dve, s_feat if k == 0 else s_fin, a)
                    shape = [P, TPB, D]
                    dve.tensor_tensor(work[:], agg[s][:], columns(has_edge, a).unsqueeze(2).to_broadcast(shape),
                                      ALU.mult).then_inc(m.node_steps, 1)
                    wait(dve, m.node_steps, a * steps + 1)
                    if k == 0:
                        wait(dve, s_root1, a + 1)
                    dve.tensor_tensor(work[:], work[:], ps_root[s] if k == 0 else columns(root, a), ALU.add
                                      ).then_inc(m.node_steps, 1)
                    wait(dve, m.node_steps, a * steps + 2)
                    if k == 0:
                        wait(dve, s_feat_turned, a - 1)
                    ins = dve.scalar_tensor_tensor(out=feat[s][:], in0=work[:], scalar=SLOPE, in1=work[:],
                                                   op0=ALU.mult, op1=ALU.max)
                    if k == 0:
                        ins.then_inc(s_feat, 1)
                        if not (isinstance(a, int) and a >= NBLK - 2):
                            make_norm(a + 2)
                    else:
                        ins.then_inc(m.node_steps, 1)
                        wait(dve, m.node_steps, a * steps + 3)
                        wait(dve, s_out[s], u * 16)
                        dve.tensor_tensor(y_sb[s][:, 0:TPB], feat[s][:], columns(x_sb, a), ALU.add).then_inc(s_fin, 1)
                return step

            for s in range(2):
                dve.memset(feat_t[s][D:D + 1, :], 1.0).then_inc(s_const, 1)
            dve.memset(w_node[1][D:D + 1, 0:D], 0.0).then_inc(s_const, 1)
            dve.wait_ge(s_iota, POOL_CONSTANTS)
            dve.tensor_scalar(ident[:], iota_row[:], iota_part[:, 0:1], None, ALU.is_equal).then_inc(s_const, 1)
            dve.tensor_scalar(below[:], iota_row[:], iota_part[:, 0:1], None, ALU.is_gt).then_inc(s_const, 1)
            dve.tensor_copy(ps_iota[:, 0:P], iota_row[:]).then_inc(s_const, 1)

            def make_mask():
                dve.wait_ge(s_dst_runs, 16)
                dve.tensor_tensor(mask_sb[:], dst_seq[:, 1:ECOL + 1], dst_seq[:, 0:ECOL], ALU.is_equal).then_inc(s_mask, 1)
                dve.wait_ge(s_mask, 1)
                dve.tensor_scalar(mask_sb[:], mask_sb[:], 2.0, -1.0, ALU.mult, ALU.add).then_inc(s_mask, 1)

            split_link = chain(s_split)

            def split_partition():
                dve.wait_ge(s_dst_tiles, 16)
                dve.wait_ge(s_mask, 2)
                split_link(dve.tensor_scalar(dst_a[:], dst_i[:], 2, P - 1, ALU.logical_shift_right, ALU.bitwise_and))
                split_link(dve.tensor_copy(dst_p[:], dst_a[:]))

            def split_column():
                split_link(dve.tensor_scalar(dst_b[:], dst_i[:], 9, 2, ALU.logical_shift_right, ALU.logical_shift_left))
                split_link(dve.tensor_scalar(dst_a[:], dst_i[:], TPB - 1, None, ALU.bitwise_and))
                split_link(dve.tensor_tensor(dst_c[:], dst_a[:], dst_b[:], ALU.add))

            over_node_pairs(dve, reduce_pair)
            add_squares(NODE_PAIRS - 1, 0, 1)
            invert_std(NODE_PAIRS - 2, 2)
            scale_y(NODE_PAIRS - 2, 1, 2)
            invert_std(NODE_PAIRS - 1, 1)
            scale_y(NODE_PAIRS - 1, 0, 1)
            make_mask()
            split_partition()
            split_column()

            over_edges(dve, scan(0))
            dve.wait_ge(edges[0].hot_used, EBLK)
            find_ends()
            for a in range(2):
                make_norm(a)
            over_nodes(dve, finish(0), NBLK - 2)
            for a in (NBLK - 2, NBLK - 1):
                finish(0)(a, a % 2, a // 2)
            over_edges(dve, scan(1))
            over_nodes(dve, finish(1))


def kernel(**inputs):
    import concourse.bacc as bacc
    from concourse.bass_utils import run_bass_kernel_spmd

    a = {n: np.ascontiguousarray(v) for n, v in inputs.items()}
    x, src, dst, ea = a["x"], a["src"], a["dst"], a["edge_attr_32"]
    N, D = x.shape
    E, DE = ea.shape
    nblk, eblk = cdiv(N, BLOCK), cdiv(E, BLOCK)
    npair = cdiv(eblk, 2)

    x_pad = np.zeros((nblk * BLOCK, D), x.dtype)
    x_pad[:N] = x
    src_pad = np.zeros(npair * PAIR, src.dtype)
    src_pad[:E] = src
    dst_run = np.full(1 + eblk * BLOCK, N, dst.dtype)
    dst_run[0] = -1
    dst_run[1:E + 1] = dst
    ea_pad = np.zeros((eblk * BLOCK, DE), ea.dtype)
    ea_pad[:E] = ea
    arrays = {
        "x_pad": x_pad,
        "src_tiles": np.ascontiguousarray(src_pad.reshape(npair, 2 * TPB, P).transpose(0, 2, 1)),
        "dst_tiles": np.ascontiguousarray(dst_run[1:].reshape(eblk * TPB, P).T),
        "dst_run": np.stack([dst_run[p * eblk * TPB:(p + 1) * eblk * TPB + 1] for p in range(P)]),
        "edge_attr_t": np.ascontiguousarray(ea_pad.reshape(eblk, BLOCK, DE).transpose(0, 2, 1)),
    }
    names = [[f"L0_gnn_{w}" for w in (f"W{k}_msg", f"W{k}_edge", f"W{k}_root", f"b{k}")] for k in (1, 2)]
    arrays |= {n: a[n] for layer in names for n in layer}

    nc = bacc.Bacc("TRN2", target_bir_lowering=False, num_devices=1)
    aps = {n: nc.dram_tensor(n, v.shape, mybir.dt.from_np(v.dtype), kind="ExternalInput").ap()
           for n, v in arrays.items()}
    out = nc.dram_tensor("out", (N, D), F32, kind="ExternalOutput").ap()
    build(nc, aps["x_pad"], aps["src_tiles"], aps["dst_tiles"], aps["dst_run"], aps["edge_attr_t"],
          [[aps[n] for n in layer] for layer in names], out, N, E)
    r = run_bass_kernel_spmd(nc, [{n: v for n, v in arrays.items()}], core_ids=[0])
    return r.results[0]["out"]
```
